# Optimizing a Trainium2 kernel written in Bass

```python
import numpy as np
import jax
import jax.numpy as jnp

def _softmax(x, axis=-1):
    return jax.nn.softmax(x, axis=axis)

def _gelu(x):
    return jax.nn.gelu(x, approximate=True)

def _silu(x):
    return jax.nn.silu(x)

def _sigmoid(x):
    return jax.nn.sigmoid(x)

def _layernorm(x, axis=-1, eps=1e-05):
    m = jnp.mean(x, axis=axis, keepdims=True)
    v = jnp.var(x, axis=axis, keepdims=True)
    return (x - m) / jnp.sqrt(v + eps)

def _scatter_add(tgt, idx, src, axis=0):
    return tgt.at[idx].add(src)

def _segment_sum(src, seg, n):
    return jax.ops.segment_sum(src, seg, n)
kernel_name = 'mk_xattn_seq_d1_seqx_r4_993011'

def setup_inputs(seed: int=0):
    np.random.seed(seed)
    _w = jnp.asarray

    def _rec_inputs():
        import jax
        import jax.numpy as jnp
        _rk = jax.random.key(seed)
        x = 7.22e-05 + 1 * jax.random.normal(jax.random.fold_in(_rk, 1), (64, 128, 256), jnp.float32)
        _lenS = 128 - jax.random.randint(jax.random.fold_in(_rk, 7), (64,), 0, max(1, 128 // 4) + 1, jnp.int32)
        _lenS2 = 128 - jax.random.randint(jax.random.fold_in(_rk, 8), (64,), 0, max(1, 128 // 4) + 1, jnp.int32)
        _ctx_512P = jax.random.normal(jax.random.fold_in(_rk, 11), (64, 16, 128), jnp.float32)
        _ctx_512c = jax.random.dirichlet(jax.random.fold_in(_rk, 511), 0.3 * jnp.ones((16,), jnp.float32), (64, 128))
        _ctx_512t = jnp.einsum('bsk,bkd->bsd', _ctx_512c, _ctx_512P)
        _ctx_512t = _ctx_512t * jax.lax.rsqrt(jnp.mean(jnp.square(_ctx_512t)) + 1e-12) * 0.953939
        ctx_512 = 4.13588e-05 + 0.999923 * (_ctx_512t + 0.3 * jax.random.normal(jax.random.fold_in(_rk, 611), (64, 128, 128), jnp.float32))
        fside_BxSxS_0 = 0.000376506 + 0.999991 * jax.random.normal(jax.random.fold_in(_rk, 12), (64, 128, 128), jnp.float32)
        return (x, ctx_512, fside_BxSxS_0)
    x, ctx_512, fside_BxSxS_0 = _rec_inputs()

    def _L0_xattn_setup():
        import jax, jax.numpy as jnp
        import numpy as np
        EPS = 1e-05

        def _ln(x, g, b):
            mu = jnp.mean(x, axis=-1, keepdims=True)
            var = jnp.var(x, axis=-1, keepdims=True)
            return (x - mu) * jax.lax.rsqrt(var + EPS) * g + b

        def _cma(x1, x2, ln1_g, ln1_b, ln2_g, ln2_b, Wq, bq, Wk, bk, Wv, bv, Wo, bo):
            e = Wq.shape[1]
            scale = e ** (-0.5)
            x1n = _ln(x1, ln1_g, ln1_b)
            x2n = _ln(x2, ln2_g, ln2_b)
            q = x1n @ Wq + bq
            k = x2n @ Wk + bk
            v = x2n @ Wv + bv
            attn = jax.nn.softmax(jnp.einsum('bqe,bke->bqk', q, k) * scale, axis=-1)
            ctx = jnp.einsum('bqk,bke->bqe', attn, v)
            return ctx @ Wo + bo
        key = jax.random.key(seed)
        ks = jax.random.split(key, 24)
        B, Lt, La, Lv = (16, 128, 256, 128)
        Dt, Da, Dv, E = (256, 128, 128, 256)
        s = lambda k, *sh: jax.random.normal(k, sh, dtype=jnp.float32) * 0.02
        inp = {'text': jax.random.normal(ks[0], (B, Lt, Dt), dtype=jnp.float32), 'audio': jax.random.normal(ks[1], (B, La, Da), dtype=jnp.float32), 'video': jax.random.normal(ks[2], (B, Lv, Dv), dtype=jnp.float32), 'a_ln1_g': jnp.ones((Dt,)), 'a_ln1_b': jnp.zeros((Dt,)), 'a_ln2_g': jnp.ones((Da,)), 'a_ln2_b': jnp.zeros((Da,)), 'a_Wq': s(ks[3], Dt, E), 'a_bq': jnp.zeros((E,)), 'a_Wk': s(ks[4], Da, E), 'a_bk': jnp.zeros((E,)), 'a_Wv': s(ks[5], Da, E), 'a_bv': jnp.zeros((E,)), 'a_Wo': s(ks[6], E, Dt), 'a_bo': jnp.zeros((Dt,)), 'v_ln1_g': jnp.ones((Dt,)), 'v_ln1_b': jnp.zeros((Dt,)), 'v_ln2_g': jnp.ones((Dv,)), 'v_ln2_b': jnp.zeros((Dv,)), 'v_Wq': s(ks[7], Dt, E), 'v_bq': jnp.zeros((E,)), 'v_Wk': s(ks[8], Dv, E), 'v_bk': jnp.zeros((E,)), 'v_Wv': s(ks[9], Dv, E), 'v_bv': jnp.zeros((E,)), 'v_Wo': s(ks[10], E, Dt), 'v_bo': jnp.zeros((Dt,)), 'ln_g': jnp.ones((Dt,)), 'ln_b': jnp.zeros((Dt,)), 'fc_W': s(ks[11], Dt, Dt), 'fc_b': jnp.zeros((Dt,))}
        return inp
    _L0_xattn_all = _L0_xattn_setup()
    _L0_xattn_in = {k: v for k, v in _L0_xattn_all.items() if k in ('a_ln1_g', 'a_ln1_b', 'a_ln2_g', 'a_ln2_b', 'a_Wq', 'a_bq', 'a_Wk', 'a_bk', 'a_Wv', 'a_bv', 'a_Wo', 'a_bo', 'v_ln1_g', 'v_ln1_b', 'v_ln2_g', 'v_ln2_b', 'v_Wq', 'v_bq', 'v_Wk', 'v_bk', 'v_Wv', 'v_bv', 'v_Wo', 'v_bo', 'ln_g', 'ln_b', 'fc_W', 'fc_b')}
    del _L0_xattn_all
    return {'x': x, 'ctx_512': ctx_512, 'fside_BxSxS_0': fside_BxSxS_0, 'L0_xattn_a_ln1_g': _L0_xattn_in['a_ln1_g'], 'L0_xattn_a_ln1_b': _L0_xattn_in['a_ln1_b'], 'L0_xattn_a_ln2_g': _L0_xattn_in['a_ln2_g'], 'L0_xattn_a_ln2_b': _L0_xattn_in['a_ln2_b'], 'L0_xattn_a_Wq': _L0_xattn_in['a_Wq'], 'L0_xattn_a_bq': _L0_xattn_in['a_bq'], 'L0_xattn_a_Wk': _L0_xattn_in['a_Wk'], 'L0_xattn_a_bk': _L0_xattn_in['a_bk'], 'L0_xattn_a_Wv': _L0_xattn_in['a_Wv'], 'L0_xattn_a_bv': _L0_xattn_in['a_bv'], 'L0_xattn_a_Wo': _L0_xattn_in['a_Wo'], 'L0_xattn_a_bo': _L0_xattn_in['a_bo'], 'L0_xattn_v_ln1_g': _L0_xattn_in['v_ln1_g'], 'L0_xattn_v_ln1_b': _L0_xattn_in['v_ln1_b'], 'L0_xattn_v_ln2_g': _L0_xattn_in['v_ln2_g'], 'L0_xattn_v_ln2_b': _L0_xattn_in['v_ln2_b'], 'L0_xattn_v_Wq': _L0_xattn_in['v_Wq'], 'L0_xattn_v_bq': _L0_xattn_in['v_bq'], 'L0_xattn_v_Wk': _L0_xattn_in['v_Wk'], 'L0_xattn_v_bk': _L0_xattn_in['v_bk'], 'L0_xattn_v_Wv': _L0_xattn_in['v_Wv'], 'L0_xattn_v_bv': _L0_xattn_in['v_bv'], 'L0_xattn_v_Wo': _L0_xattn_in['v_Wo'], 'L0_xattn_v_bo': _L0_xattn_in['v_bo'], 'L0_xattn_ln_g': _L0_xattn_in['ln_g'], 'L0_xattn_ln_b': _L0_xattn_in['ln_b'], 'L0_xattn_fc_W': _L0_xattn_in['fc_W'], 'L0_xattn_fc_b': _L0_xattn_in['fc_b']}

def reference(x, ctx_512, fside_BxSxS_0, L0_xattn_a_ln1_g, L0_xattn_a_ln1_b, L0_xattn_a_ln2_g, L0_xattn_a_ln2_b, L0_xattn_a_Wq, L0_xattn_a_bq, L0_xattn_a_Wk, L0_xattn_a_bk, L0_xattn_a_Wv, L0_xattn_a_bv, L0_xattn_a_Wo, L0_xattn_a_bo, L0_xattn_v_ln1_g, L0_xattn_v_ln1_b, L0_xattn_v_ln2_g, L0_xattn_v_ln2_b, L0_xattn_v_Wq, L0_xattn_v_bq, L0_xattn_v_Wk, L0_xattn_v_bk, L0_xattn_v_Wv, L0_xattn_v_bv, L0_xattn_v_Wo, L0_xattn_v_bo, L0_xattn_ln_g, L0_xattn_ln_b, L0_xattn_fc_W, L0_xattn_fc_b):
    import jax
    import jax.numpy as jnp

    def _L0_xattn_ref(text, audio, video, a_ln1_g, a_ln1_b, a_ln2_g, a_ln2_b, a_Wq, a_bq, a_Wk, a_bk, a_Wv, a_bv, a_Wo, a_bo, v_ln1_g, v_ln1_b, v_ln2_g, v_ln2_b, v_Wq, v_bq, v_Wk, v_bk, v_Wv, v_bv, v_Wo, v_bo, ln_g, ln_b, fc_W, fc_b):
        import jax, jax.numpy as jnp
        import numpy as np
        EPS = 1e-05

        def _ln(x, g, b):
            mu = jnp.mean(x, axis=-1, keepdims=True)
            var = jnp.var(x, axis=-1, keepdims=True)
            return (x - mu) * jax.lax.rsqrt(var + EPS) * g + b

        def _cma(x1, x2, ln1_g, ln1_b, ln2_g, ln2_b, Wq, bq, Wk, bk, Wv, bv, Wo, bo):
            e = Wq.shape[1]
            scale = e ** (-0.5)
            x1n = _ln(x1, ln1_g, ln1_b)
            x2n = _ln(x2, ln2_g, ln2_b)
            q = x1n @ Wq + bq
            k = x2n @ Wk + bk
            v = x2n @ Wv + bv
            attn = jax.nn.softmax(jnp.einsum('bqe,bke->bqk', q, k) * scale, axis=-1)
            ctx = jnp.einsum('bqk,bke->bqe', attn, v)
            return ctx @ Wo + bo
        out_a = _cma(text, audio, a_ln1_g, a_ln1_b, a_ln2_g, a_ln2_b, a_Wq, a_bq, a_Wk, a_bk, a_Wv, a_bv, a_Wo, a_bo)
        out_v = _cma(text, video, v_ln1_g, v_ln1_b, v_ln2_g, v_ln2_b, v_Wq, v_bq, v_Wk, v_bk, v_Wv, v_bv, v_Wo, v_bo)
        output = out_a + out_v + text
        residual = output
        output = _ln(output, ln_g, ln_b) @ fc_W + fc_b
        return output + residual
    x = _L0_xattn_ref(x, ctx_512, fside_BxSxS_0, L0_xattn_a_ln1_g, L0_xattn_a_ln1_b, L0_xattn_a_ln2_g, L0_xattn_a_ln2_b, L0_xattn_a_Wq, L0_xattn_a_bq, L0_xattn_a_Wk, L0_xattn_a_bk, L0_xattn_a_Wv, L0_xattn_a_bv, L0_xattn_a_Wo, L0_xattn_a_bo, L0_xattn_v_ln1_g, L0_xattn_v_ln1_b, L0_xattn_v_ln2_g, L0_xattn_v_ln2_b, L0_xattn_v_Wq, L0_xattn_v_bq, L0_xattn_v_Wk, L0_xattn_v_bk, L0_xattn_v_Wv, L0_xattn_v_bv, L0_xattn_v_Wo, L0_xattn_v_bo, L0_xattn_ln_g, L0_xattn_ln_b, L0_xattn_fc_W, L0_xattn_fc_b)
    return x

_drawn_inputs = setup_inputs


def setup_inputs(seed=0):
    import zlib

    import numpy as np

    out = dict(_drawn_inputs(seed))
    spreads = {'L0_xattn_a_ln1_g': (1.0, 0.6),
     'L0_xattn_a_ln1_b': (0.0, 0.8),
     'L0_xattn_a_ln2_g': (1.0, 0.6),
     'L0_xattn_a_ln2_b': (0.0, 0.8),
     'L0_xattn_a_bq': (0.0, 2.0),
     'L0_xattn_a_bk': (0.0, 2.0),
     'L0_xattn_a_bv': (0.0, 0.291),
     'L0_xattn_a_bo': (0.0, 0.1),
     'L0_xattn_v_ln1_g': (1.0, 0.6),
     'L0_xattn_v_ln1_b': (0.0, 0.8),
     'L0_xattn_v_ln2_g': (1.0, 0.6),
     'L0_xattn_v_ln2_b': (0.0, 0.8),
     'L0_xattn_v_bq': (0.0, 0.8),
     'L0_xattn_v_bk': (0.0, 2.0),
     'L0_xattn_v_bv': (0.0, 0.296),
     'L0_xattn_v_bo': (0.0, 0.1),
     'L0_xattn_ln_g': (1.0, 0.2),
     'L0_xattn_ln_b': (0.0, 0.304),
     'L0_xattn_fc_b': (0.0, 0.1)}
    factors = {'fside_BxSxS_0': 8.0,
     'L0_xattn_a_Wq': 8.0,
     'L0_xattn_a_Wk': 8.0,
     'L0_xattn_v_Wq': 8.0,
     'L0_xattn_v_Wk': 8.0,
     'L0_xattn_v_Wv': 6.24}
    for name, (base, spread) in spreads.items():
        noise = np.random.default_rng([zlib.crc32(name.encode()), seed]).standard_normal(out[name].shape)
        drawn = base * np.exp(spread * noise) if base else spread * noise
        out[name] = jnp.asarray(drawn.astype(out[name].dtype))
    for name, factor in factors.items():
        out[name] = (out[name] * factor).astype(out[name].dtype)
    return out
```

```python
import concourse.bass as bass
from concourse import mybir
from contextlib import ExitStack

FP32 = mybir.dt.float32
F32R = mybir.dt.float32r
ALU = mybir.AluOpType
ACT = mybir.ActivationFunctionType
AX = mybir.AxisListType

EPS = 1e-5
P = 128
RING = 4


def xattn_kernel(nc, x, ctx_in, fside, wq_a, wk_a, wv_a, wo_a, wq_v, wk_v, wv_v, wo_v, fc_w,
                 norm_cols, bias_rows, out):
    B, S, DT = x.shape
    E = wq_a.shape[1]
    KT = DT // P
    KE = E // P
    PAIRS = B // 2
    SCALE = float(E) ** -0.5
    NCOL = 8
    LN1, LN2, LNF = (0, 3), (2, 5), 6
    BQ, BK, BV, BO, BFC = (0, 4), (1, 5), (2, 6), (3, 7), 8

    x_pairs = x.rearrange("(p b) s d -> p s b d", b=2)
    c_pairs = ctx_in.rearrange("(p b) s d -> p s b d", b=2)
    f_pairs = fside.rearrange("(p b) s d -> p s b d", b=2)
    out_pairs = out.rearrange("(p b) s d -> p s b d", b=2)

    es = ExitStack()
    with es:
        def sb(name, shape, dt=FP32):
            return es.enter_context(nc.sbuf_tensor(name, shape, dt))

        def pb(name):
            return es.enter_context(nc.psum_tensor(name, [P, 512], FP32))

        def sem(name):
            return es.enter_context(nc.semaphore(name))

        ident = sb("ident", [P, P])
        mean_dt = sb("mean_dt", [P, P])
        mean_dc = sb("mean_dc", [P, P])
        minus_half = sb("minus_half", [P, 6])
        eps = sb("eps", [P, 6])
        one = sb("one", [P, 6])
        cols = sb("cols", [P, 2 * NCOL])
        shift_less_gain = sb("shift_less_gain", [P, NCOL])
        rows = sb("rows", [1, 9, E])
        wq = sb("wq", [P, 2, KT, E])
        wk = sb("wk", [P, 2, E])
        wv = sb("wv", [P, 2, E])
        wo = sb("wo", [P, 2, KE, DT])
        wf = sb("wf", [P, KT, DT])
        q2 = sb("q2", [P, 2, KT, E])
        k2 = sb("k2", [P, 2, E])
        v2 = sb("v2", [P, 2, E])
        f2 = sb("f2", [P, KT, DT])
        q2T = sb("q2T", [P, 2, KE, DT])
        kv2T = sb("kv2T", [P, 2, 2, KE, P])
        m_hi = sb("m_hi", [P, 2, KT, P], F32R)
        m_lo = sb("m_lo", [P, 2, KT, P], F32R)
        o_hi = sb("o_hi", [P, 2, DT], F32R)
        o_lo = sb("o_lo", [P, 2, DT], F32R)
        f_hi = sb("f_hi", [P, KT, DT], F32R)
        f_lo = sb("f_lo", [P, KT, DT], F32R)

        x_all = sb("x_all", [P, PAIRS, 2, DT])
        scaled = x_all[:, PAIRS - 5:PAIRS, :, :].rearrange("p a b d -> p (a b) d")
        raw = sb("raw", [P, RING, 2, 2, P])
        cn = sb("cn", [P, RING, 2, 2, P])
        y = sb("y", [P, RING, 2, DT])
        in_bn = sb("in_bn", [P, 2, 6, 6])
        in_mv = sb("in_mv", [P, 2, 6, 2])
        in_var_eps = sb("in_var_eps", [P, 2, 6])
        in_rstd = sb("in_rstd", [P, 2, 6])
        in_mean_rstd = sb("in_mean_rstd", [P, 2, 6])
        in_offset = sb("in_offset", [P, 2, 6])
        y_bn = sb("y_bn", [P, 2, 2, 6])
        y_mv = sb("y_mv", [P, 2, 2, 2])
        y_var_eps = sb("y_var_eps", [P, 2, 2])
        y_rstd = sb("y_rstd", [P, 2, 2])
        y_mean_rstd = sb("y_mean_rstd", [P, 2, 2])
        y_offset = sb("y_offset", [P, 2, 2])
        xn = sb("xn", [P, 2, 2, DT])
        xT_hi = [sb(f"xT_hi{s}", [P, KT, 2 * P], F32R) for s in range(2)]
        xT_lo = [sb(f"xT_lo{s}", [P, KT, 2 * P], F32R) for s in range(2)]
        cT = sb("cT", [P, 2, 2, 2, P])
        uT = sb("uT", [P, 2, 2, 2, P])
        neg_max = sb("neg_max", [P, 2, 4])
        exps = sb("exps", [P, 2, 4, P])
        exp_sum = sb("exp_sum", [P, 2, 4])
        inv_sum = sb("inv_sum", [P, 2, 4])
        attn = sb("attn", [P, 2, 4, P])
        attnT = sb("attnT", [P, 2, 4, P])
        acT_hi = [sb(f"acT_hi{s}", [P, 4, P], F32R) for s in range(2)]
        acT_lo = [sb(f"acT_lo{s}", [P, 4, P], F32R) for s in range(2)]
        yn = sb("yn", [P, 2, 2, DT])
        yT_hi = [sb(f"yT_hi{s}", [P, KT, 2, P], F32R) for s in range(2)]
        yT_lo = [sb(f"yT_lo{s}", [P, KT, 2, P], F32R) for s in range(2)]
        result = sb("result", [P, 2, 2, DT])

        bank_xT, bank_cT, bank_s, bank_pT = pb("bank_xT"), pb("bank_cT"), pb("bank_s"), pb("bank_pT")
        bank_ac, bank_u, bank_y, bank_f = pb("bank_ac"), pb("bank_u"), pb("bank_y"), pb("bank_f")

        ident_made, consts_made, half_made = sem("ident_made"), sem("consts_made"), sem("half_made")
        cols_in, rows_in = sem("cols_in"), sem("rows_in")
        wq_in, wk_in, wv_in, wo_in, wf_in = (sem(n) for n in ("wq_in", "wk_in", "wv_in", "wo_in", "wf_in"))
        diff_made, scaled_made, folded = sem("diff_made"), sem("scaled_made"), sem("folded")
        means_made, turned, turned_out = sem("means_made"), sem("turned"), sem("turned_out")
        m_made, o_made = sem("m_made"), sem("o_made")
        hi_made, lo_made = sem("hi_made"), sem("lo_made")

        loaded = [sem(f"loaded{s}") for s in range(RING)]
        stored = [sem(f"stored{s}") for s in range(2)]
        in_bn_done, in_mv_done = sem("in_bn_done"), sem("in_mv_done")
        in_var_done, in_rstd_done = sem("in_var_done"), sem("in_rstd_done")
        in_prod_done, in_norm_ready = sem("in_prod_done"), sem("in_norm_ready")
        y_bn_done, y_mv_done = sem("y_bn_done"), sem("y_mv_done")
        y_var_done, y_rstd_done = sem("y_var_done"), sem("y_rstd_done")
        y_prod_done, y_norm_ready = sem("y_prod_done"), sem("y_norm_ready")
        xn_ready, cn_ready, yn_ready = sem("xn_ready"), sem("cn_ready"), sem("yn_ready")
        xT_done, cT_done, s_done, pT_done = sem("xT_done"), sem("cT_done"), sem("s_done"), sem("pT_done")
        ac_done, u_done, y_done, yT_done, f_done = (sem(n) for n in (
            "ac_done", "u_done", "y_done", "yT_done", "f_done"))
        xhi_ready, xlo_ready, cT_ready, uT_ready = (sem(n) for n in (
            "xhi_ready", "xlo_ready", "cT_ready", "uT_ready"))
        max_ready, exp_ready, inv_ready, attn_ready = (sem(n) for n in (
            "max_ready", "exp_ready", "inv_ready", "attn_ready"))
        attnT_ready, achi_ready, aclo_ready = sem("attnT_ready"), sem("achi_ready"), sem("aclo_ready")
        y_ready, yhi_ready, ylo_ready, out_ready = (sem(n) for n in (
            "y_ready", "yhi_ready", "ylo_ready", "out_ready"))

        def is_pair(p):
            return not isinstance(p, int) or 0 <= p < PAIRS

        def wait_pairs(eng, semaphore, count):
            if not isinstance(count, int) or count > 0:
                eng.wait_ge(semaphore, count)

        def run_periods(eng, period, behind, ahead, skip=0):
            first = behind + skip
            rounds = (PAIRS - ahead - first) // RING
            after = first + rounds * RING
            for t in range(-ahead, first):
                period(t, t)
            with eng.Fori(first, after - RING + 1, RING) as base:
                for j in range(RING):
                    period(base + j, first + j)
            for t in range(after, PAIRS + behind):
                period(t, t)

        folds = []
        for a in range(2):
            folds += [(lambda k, a=a: wq[:, a, k, :], KT, mean_dt, lambda k, a=a: q2[:, a, k, :], LN1[a], BQ[a], wq_in, 32),
                      (lambda k, a=a: wk[:, a, :], 1, mean_dc, lambda k, a=a: k2[:, a, :], LN2[a], BK[a], wk_in, 32),
                      (lambda k, a=a: wv[:, a, :], 1, mean_dc, lambda k, a=a: v2[:, a, :], LN2[a], BV[a], wv_in, 32)]
        folds.append((lambda k: wf[:, k, :], KT, mean_dt, lambda k: f2[:, k, :], LNF, BFC, wf_in, 16))
        mean_banks = [bank_xT, bank_cT, bank_s, bank_pT, bank_ac, bank_u, bank_y]
        turned_banks = ((bank_xT, bank_cT), (bank_s, bank_pT))
        bank_m, bank_o = bank_ac, bank_u

        def means(i):
            return mean_banks[i][:, 0:E]

        first_chunk = [sum(f[1] for f in folds[:i]) for i in range(len(folds))]

        block = es.enter_context(nc.Block())

        @block.sync
        def _(sp):
            sp.dma_start(cols[:, :], norm_cols).then_inc(cols_in, 16)
            sp.dma_start(rows[:, :, :], bias_rows).then_inc(rows_in, 16)
            for a, w in enumerate((wq_a, wq_v)):
                sp.dma_start(wq[:, a, :, :], w.rearrange("(k p) e -> p k e", p=P)).then_inc(wq_in, 16)
            for a, w in enumerate((wk_a, wk_v)):
                sp.dma_start(wk[:, a, :], w).then_inc(wk_in, 16)
            for a, w in enumerate((wv_a, wv_v)):
                sp.dma_start(wv[:, a, :], w).then_inc(wv_in, 16)

            def load(p, s):
                wait_pairs(sp, cn_ready, p - RING + 1)
                arrived = loaded[s % RING]
                sp.dma_start(x_all[:, bass.ds(p, 1), :, :], x_pairs[bass.ds(p, 1)].rearrange("p s b d -> s p b d")).then_inc(arrived, 16)
                sp.dma_start(raw[:, s % RING, 0, :, :], c_pairs[bass.ds(p, 1)].rearrange("p s b d -> s (p b) d")).then_inc(arrived, 16)
                sp.dma_start(raw[:, s % RING, 1, :, :], f_pairs[bass.ds(p, 1)].rearrange("p s b d -> s (p b) d")).then_inc(arrived, 16)

            def period(t, s):
                if is_pair(t - 4):
                    sp.wait_ge(out_ready, t - 4 + 1)
                    sp.dma_start(out_pairs[bass.ds(t - 4, 1)].rearrange("p s b d -> s (p b) d"),
                                 result[:, s % 2, :, :]).then_inc(stored[s % 2], 16)
                if is_pair(t + 5):
                    load(t + 5, s + 5)
                if isinstance(t, int) and t == -4:
                    for a, w in enumerate((wo_a, wo_v)):
                        sp.dma_start(wo[:, a, :, :], w.rearrange("(k p) d -> p k d", p=P)).then_inc(wo_in, 16)
                    sp.dma_start(wf[:, :, :], fc_w.rearrange("(k p) d -> p k d", p=P)).then_inc(wf_in, 16)

            run_periods(sp, period, 4, 5)
            for s in range(2):
                sp.wait_ge(stored[s], 16 * (PAIRS // 2))

        @block.gpsimd
        def _(pool):
            pool.memset(ident[:, :], 0.0).then_inc(ident_made, 1)
            pool.memset(eps[:, :], EPS)
            pool.memset(one[:, :], 1.0)
            pool.memset(minus_half[:, :], -0.5).then_inc(half_made, 1)
            pool.wait_ge(ident_made, 1)
            pool.affine_select(out=ident[:, :], in_=ident[:, :], compare_op=ALU.not_equal, fill=1.0,
                               base=0, pattern=[[-1, P]], channel_multiplier=1).then_inc(ident_made, 1)

            def norm_scalars(p, mv, mv_done, var_eps, var_done, rstd, rstd_done, prod, prod_done, offset, ready):
                pool.wait_ge(mv_done, p + 1)
                rows = var_eps.shape[1]
                pool.tensor_tensor(var_eps, mv[:, :, 1], eps[:, 0:rows], ALU.add).then_inc(var_done, 1)
                pool.wait_ge(var_done, p + 1)
                pool.tensor_tensor(rstd, var_eps, minus_half[:, 0:rows], ALU.pow).then_inc(rstd_done, 1)
                pool.wait_ge(rstd_done, p + 1)
                pool.tensor_tensor(prod, mv[:, :, 0], rstd, ALU.mult).then_inc(prod_done, 1)
                pool.wait_ge(prod_done, p + 1)
                pool.tensor_tensor(offset, one[:, 0:rows], prod, ALU.subtract).then_inc(ready, 1)

            pool.wait_ge(half_made, 1)

            def period(t, s):
                if is_pair(t + 2):
                    p, w = t + 2, s % 2
                    wait_pairs(pool, xn_ready, p - 1)
                    norm_scalars(p, in_mv[:, w], in_mv_done, in_var_eps[:, w], in_var_done, in_rstd[:, w],
                                 in_rstd_done, in_mean_rstd[:, w], in_prod_done, in_offset[:, w], in_norm_ready)
                    pool.wait_ge(in_norm_ready, p + 1)
                    wait_pairs(pool, ac_done, p - 3)
                if is_pair(t - 2):
                    w = s % 2
                    norm_scalars(t - 2, y_mv[:, w], y_mv_done, y_var_eps[:, w], y_var_done, y_rstd[:, w],
                                 y_rstd_done, y_mean_rstd[:, w], y_prod_done, y_offset[:, w], y_norm_ready)
                if is_pair(t + 2):
                    w, r = s % 2, (s + 2) % RING
                    for a in range(2):
                        for b in range(2):
                            i = 2 + 2 * a + b
                            last = pool.tensor_scalar(cn[:, r, a, b, :], raw[:, r, a, b, :], in_rstd[:, w, i:i + 1],
                                                      in_offset[:, w, i:i + 1], ALU.mult, ALU.add)
                    last.then_inc(cn_ready, 1)
                if is_pair(t):
                    w = s % 2
                    pool.wait_ge(inv_ready, t + 1)
                    wait_pairs(pool, pT_done, t - 1)
                    pool.tensor_tensor(attn[:, w], exps[:, w], inv_sum[:, w].unsqueeze(2).to_broadcast([P, 4, P]),
                                       ALU.mult).then_inc(attn_ready, 1)

            run_periods(pool, period, 2, 2)

        @block.scalar
        def _(act):
            for i, (src, dst) in enumerate((bank, into[:, a]) for a in range(2)
                                           for bank, into in zip(turned_banks[a], (q2T, kv2T))):
                act.wait_ge(turned, i + 1)
                act.activation(flat(dst), src[:, :], ACT.Copy).then_inc(turned_out, 1)
            act.wait_ge(m_made, 1)
            act.activation(flat(m_hi), bank_m[:, :], ACT.Copy, scale=SCALE).then_inc(hi_made, 1)
            act.wait_ge(o_made, 1)
            act.activation(flat(o_hi), bank_o[:, :], ACT.Copy).then_inc(hi_made, 1)
            act.wait_ge(folded, len(folds))
            act.activation(flat(f_hi), flat(f2), ACT.Copy).then_inc(hi_made, 1)

            def period(t, s):
                w, v = s % 2, (s + 1) % 2
                if is_pair(t - 3):
                    act.wait_ge(yT_done, t - 3 + 1)
                    act.activation(flat(yT_hi[v]), bank_f[:, :], ACT.Copy).then_inc(yhi_ready, 1)
                if is_pair(t + 1):
                    act.wait_ge(xT_done, t + 1 + 1)
                    wait_pairs(act, u_done, t + 1 - 1)
                    act.activation(flat(xT_hi[v]), bank_xT[:, :], ACT.Copy).then_inc(xhi_ready, 1)
                    act.wait_ge(cT_done, t + 1 + 1)
                    wait_pairs(act, s_done, t + 1 - 1)
                    act.activation(flat(cT[:, v]), bank_cT[:, :], ACT.Copy).then_inc(cT_ready, 1)
                if is_pair(t - 1):
                    act.wait_ge(pT_done, t - 1 + 1)
                    wait_pairs(act, ac_done, t - 1 - 1)
                    act.activation(flat(attnT[:, v]), bank_pT[:, :], ACT.Copy).then_inc(attnT_ready, 1)
                if is_pair(t - 2):
                    act.wait_ge(y_norm_ready, t - 2 + 1)
                    for b in range(2):
                        last = act.activation(yn[:, w, b, :], y[:, (s - 2) % RING, b, :], ACT.Identity,
                                              bias=y_offset[:, w, b:b + 1], scale=y_rstd[:, w, b:b + 1])
                    last.then_inc(yn_ready, 1)
                if is_pair(t - 1):
                    act.wait_ge(ac_done, t - 1 + 1)
                    wait_pairs(act, y_done, t - 1 - 1)
                    act.activation(flat(acT_hi[v]), bank_ac[:, :], ACT.Copy).then_inc(achi_ready, 1)
                if is_pair(t):
                    act.wait_ge(max_ready, t + 1)
                    wait_pairs(act, attn_ready, t - 1)
                    for i in range(4):
                        last = act.activation(exps[:, w, i, :], bank_s[:, i * P:(i + 1) * P], ACT.Exp,
                                              bias=neg_max[:, w, i:i + 1], accum_out=exp_sum[:, w, i:i + 1])
                    last.then_inc(exp_ready, 1)
                if is_pair(t + 1):
                    act.wait_ge(u_done, t + 1 + 1)
                    wait_pairs(act, s_done, t + 1 - 1)
                    act.activation(flat(uT[:, v]), bank_u[:, :], ACT.Copy).then_inc(uT_ready, 1)
                if is_pair(t + 2):
                    act.wait_ge(in_norm_ready, t + 2 + 1)
                    wait_pairs(act, xT_done, t + 2 - 1)
                    for b in range(2):
                        last = act.activation(xn[:, w, b, :], x_all[:, bass.ds(t + 2, 1), b, :], ACT.Identity,
                                              bias=in_offset[:, w, b:b + 1], scale=in_rstd[:, w, b:b + 1])
                    last.then_inc(xn_ready, 1)

            run_periods(act, period, 3, 2)

        @block.vector
        def _(dve):
            dve.memset(mean_dt[:, :], 1.0 / DT)
            dve.memset(mean_dc[:, :], 1.0 / P).then_inc(consts_made, 1)
            dve.wait_ge(cols_in, 16)
            dve.tensor_tensor(shift_less_gain[:, :], cols[:, NCOL:2 * NCOL], cols[:, 0:NCOL],
                              ALU.subtract).then_inc(diff_made, 1)
            dve.wait_ge(diff_made, 1)

            def scale_weight(i):
                weight, chunks, _, _, norm, _, arrived, full = folds[i]
                dve.wait_ge(arrived, full)
                for k in range(chunks):
                    last = dve.tensor_scalar(scaled[:, first_chunk[i] + k, :], weight(k),
                                             shift_less_gain[:, norm + k:norm + k + 1], None, ALU.mult)
                last.then_inc(scaled_made, 1)

            def fold_weight(i):
                weight, chunks, _, folded_weight, norm, _, _, _ = folds[i]
                dve.wait_ge(means_made, i + 1)
                for k in range(chunks):
                    last = dve.scalar_tensor_tensor(folded_weight(k), weight(k), cols[:, norm + k:norm + k + 1],
                                                    means(i), ALU.mult, ALU.add)
                last.then_inc(folded, 1)

            for i in range(len(folds)):
                scale_weight(i)
                if i >= 1:
                    fold_weight(i - 1)
            fold_weight(len(folds) - 1)
            dve.wait_ge(hi_made, 1)
            dve.scalar_tensor_tensor(flat(m_lo), bank_m[:, :], SCALE, flat(m_hi).bitcast(FP32),
                                     ALU.mult, ALU.subtract).then_inc(lo_made, 1)
            dve.wait_ge(hi_made, 2)
            dve.tensor_tensor(flat(o_lo), bank_o[:, :], flat(o_hi).bitcast(FP32), ALU.subtract).then_inc(lo_made, 1)
            dve.wait_ge(hi_made, 3)
            dve.tensor_tensor(flat(f_lo), flat(f2), flat(f_hi).bitcast(FP32), ALU.subtract).then_inc(lo_made, 1)

            def period(t, s):
                w, v, r = s % 2, (s + 1) % 2, s % RING
                if is_pair(t - 2):
                    dve.wait_ge(y_bn_done, t - 2 + 1)
                    wait_pairs(dve, y_norm_ready, t - 2 - 1)
                if is_pair(t - 4):
                    p = t - 4
                    dve.wait_ge(f_done, p + 1)
                    wait_pairs(dve, stored[w], 8 * (p - w))
                    dve.tensor_tensor(flat(result[:, w]), bank_f[:, :], flat(y[:, r]), ALU.add).then_inc(out_ready, 1)
                if is_pair(t - 2):
                    for b in range(2):
                        last = dve.bn_aggr(y_mv[:, w, b, :], y_bn[:, w, b, :])
                    last.then_inc(y_mv_done, 1)
                if is_pair(t + 1):
                    dve.wait_ge(xhi_ready, t + 1 + 1)
                    dve.tensor_tensor(flat(xT_lo[v]), bank_xT[:, :], flat(xT_hi[v]).bitcast(FP32),
                                      ALU.subtract).then_inc(xlo_ready, 1)
                if is_pair(t - 3):
                    dve.wait_ge(yhi_ready, t - 3 + 1)
                    dve.tensor_tensor(flat(yT_lo[v]), bank_f[:, :], flat(yT_hi[v]).bitcast(FP32),
                                      ALU.subtract).then_inc(ylo_ready, 1)
                if is_pair(t):
                    dve.wait_ge(s_done, t + 1)
                    wait_pairs(dve, exp_ready, t - 1)
                    dve.tensor_reduce(neg_max[:, w], bank_s[:, :].rearrange("p (i k) -> p i k", i=4), AX.X, ALU.max,
                                      negate=True).then_inc(max_ready, 1)
                if is_pair(t + 3):
                    dve.wait_ge(loaded[(s + 3) % RING], 12 * (t + 3 - (s + 3) % RING) + 48)
                    for b in range(2):
                        dve.bn_stats(in_bn[:, v, b, :], x_all[:, bass.ds(t + 3, 1), b, :])
                if is_pair(t - 1):
                    dve.wait_ge(achi_ready, t - 1 + 1)
                    dve.tensor_tensor(flat(acT_lo[v]), bank_ac[:, :], flat(acT_hi[v]).bitcast(FP32),
                                      ALU.subtract).then_inc(aclo_ready, 1)
                if is_pair(t + 3):
                    for i in range(4):
                        last = dve.bn_stats(in_bn[:, v, 2 + i, :], raw[:, (s + 3) % RING, i // 2, i % 2, :])
                    last.then_inc(in_bn_done, 1)
                    wait_pairs(dve, in_norm_ready, t + 3 - 1)
                    dve.wait_ge(in_bn_done, t + 3 + 1)
                if is_pair(t):
                    dve.wait_ge(exp_ready, t + 1)
                    wait_pairs(dve, attn_ready, t - 1)
                    dve.reciprocal(inv_sum[:, w], exp_sum[:, w]).then_inc(inv_ready, 1)
                if is_pair(t + 3):
                    for i in range(6):
                        last = dve.bn_aggr(in_mv[:, v, i, :], in_bn[:, v, i, :])
                    last.then_inc(in_mv_done, 1)
                if is_pair(t - 1):
                    p = t - 1
                    dve.wait_ge(y_done, p + 1)
                    dve.tensor_tensor(y[:, (s - 1) % RING], bank_y[:, :].rearrange("p (b d) -> p b d", b=2),
                                      x_all[:, bass.ds(p, 1), :, :].rearrange("p o b d -> p (o b) d"),
                                      ALU.add).then_inc(y_ready, 1)
                    dve.wait_ge(y_ready, p + 1)
                    for b in range(2):
                        last = dve.bn_stats(y_bn[:, v, b, :], y[:, (s - 1) % RING, b, :])
                    last.then_inc(y_bn_done, 1)

            run_periods(dve, period, 4, 3, skip=2)

        @block.tensor
        def _(pe):
            pe.wait_ge(consts_made, 1)
            pe.wait_ge(rows_in, 16)

            def column_means(i):
                _, chunks, mean, _, _, bias, _, _ = folds[i]
                pe.wait_ge(scaled_made, i + 1)
                for k in range(chunks):
                    pe.matmul(means(i), mean[:, :], scaled[:, first_chunk[i] + k, :], start=(k == 0), stop=False)
                pe.matmul(means(i), mean[0:1, :], rows[0:1, bias, :], start=False, stop=True).then_inc(means_made, 1)

            for i in range(len(folds)):
                column_means(i)
            pe.wait_ge(ident_made, 2)
            for a, (q_bank, kv_bank) in enumerate(turned_banks):
                pe.wait_ge(folded, (2, 4)[a])
                for e in range(KE):
                    for k in range(KT):
                        at = (e * KT + k) * P
                        last = pe.transpose(q_bank[:, at:at + P], q2[:, a, k, e * P:(e + 1) * P], ident[:, :])
                last.then_inc(turned, 1)
                pe.wait_ge(folded, 3 * a + 3)
                for i, w in enumerate((k2, v2)):
                    for e in range(KE):
                        at = (i * KE + e) * P
                        last = pe.transpose(kv_bank[:, at:at + P], w[:, a, e * P:(e + 1) * P], ident[:, :])
                last.then_inc(turned, 1)
            pe.wait_ge(turned_out, 4)
            for a in range(2):
                for k in range(KT):
                    at = (a * KT + k) * P
                    for e in range(KE):
                        last = pe.matmul(bank_m[:, at:at + P], q2T[:, a, e, k * P:(k + 1) * P], kv2T[:, a, 0, e, :],
                                         start=(e == 0), stop=(e == KE - 1))
            last.then_inc(m_made, 1)
            pe.wait_ge(wo_in, 32)
            for a in range(2):
                o = bank_o[:, a * DT:(a + 1) * DT]
                for e in range(KE):
                    pe.matmul(o, kv2T[:, a, 1, e, :], wo[:, a, e, :], start=(e == 0), stop=False)
                last = pe.matmul(o, mean_dc[0:1, :], rows[0:1, BO[a], :], start=False, stop=True)
            last.then_inc(o_made, 1)
            pe.wait_ge(folded, len(folds))
            pe.wait_ge(lo_made, 3)

            def period(t, s):
                w, v = s % 2, (s + 1) % 2
                if is_pair(t + 1):
                    p, r = t + 1, (s + 1) % RING
                    pe.wait_ge(xn_ready, p + 1)
                    wait_pairs(pe, xlo_ready, p)
                    for k in range(KT):
                        for b in range(2):
                            at = (2 * k + b) * P
                            last = pe.transpose(bank_xT[:, at:at + P], xn[:, v, b, k * P:(k + 1) * P], ident[:, :])
                    last.then_inc(xT_done, 1)
                    pe.wait_ge(cn_ready, p + 1)
                    wait_pairs(pe, cT_ready, p)
                    for a in range(2):
                        for b in range(2):
                            at = (2 * a + b) * P
                            last = pe.transpose(bank_cT[:, at:at + P], cn[:, r, a, b, :], ident[:, :])
                    last.then_inc(cT_done, 1)
                if is_pair(t - 1):
                    pe.wait_ge(attn_ready, t - 1 + 1)
                    wait_pairs(pe, attnT_ready, t - 1)
                    for i in range(4):
                        last = pe.transpose(bank_pT[:, i * P:(i + 1) * P], attn[:, v, i, :], ident[:, :])
                    last.then_inc(pT_done, 1)
                if is_pair(t):
                    pe.wait_ge(cT_ready, t + 1)
                    pe.wait_ge(uT_ready, t + 1)
                    wait_pairs(pe, exp_ready, t)
                    for a in range(2):
                        for b in range(2):
                            at = (2 * a + b) * P
                            last = pe.matmul(bank_s[:, at:at + P], uT[:, w, a, b, :], cT[:, w, a, b, :],
                                             start=True, stop=True)
                    last.then_inc(s_done, 1)
                if is_pair(t - 1):
                    pe.wait_ge(attnT_ready, t - 1 + 1)
                    wait_pairs(pe, aclo_ready, t - 1)
                    for i in range(4):
                        last = pe.matmul(bank_ac[:, i * P:(i + 1) * P], cn[:, (s - 1) % RING, i // 2, i % 2, :],
                                         attnT[:, v, i, :], start=True, stop=True)
                    last.then_inc(ac_done, 1)
                if is_pair(t + 1):
                    pe.wait_ge(xhi_ready, t + 1 + 1)
                    wait_pairs(pe, uT_ready, t + 1)
                    for a in range(2):
                        u = bank_u[:, a * 2 * P:(a + 1) * 2 * P]
                        for k in range(KT):
                            pe.matmul(u, m_hi[:, a, k, :], xT_hi[v][:, k, :], start=(k == 0), stop=False)
                            pe.matmul(u, m_lo[:, a, k, :], xT_hi[v][:, k, :], start=False, stop=False)
                        if a == 0:
                            pe.wait_ge(xlo_ready, t + 1 + 1)
                        for k in range(KT):
                            last = pe.matmul(u, m_hi[:, a, k, :], xT_lo[v][:, k, :], start=False, stop=(k == KT - 1))
                    last.then_inc(u_done, 1)
                if is_pair(t - 1):
                    pe.wait_ge(achi_ready, t - 1 + 1)
                    wait_pairs(pe, y_ready, t - 1)
                    for b in range(2):
                        o = bank_y[:, b * DT:(b + 1) * DT]
                        for a in range(2):
                            pe.matmul(o, acT_hi[v][:, 2 * a + b, :], o_hi[:, a, :], start=(a == 0), stop=False)
                            pe.matmul(o, acT_hi[v][:, 2 * a + b, :], o_lo[:, a, :], start=False, stop=False)
                        if b == 0:
                            pe.wait_ge(aclo_ready, t - 1 + 1)
                        for a in range(2):
                            last = pe.matmul(o, acT_lo[v][:, 2 * a + b, :], o_hi[:, a, :], start=False, stop=(a == 1))
                    last.then_inc(y_done, 1)
                if is_pair(t - 3):
                    pe.wait_ge(ylo_ready, t - 3 + 1)
                    for b in range(2):
                        o = bank_f[:, b * DT:(b + 1) * DT]
                        for k in range(KT):
                            pe.matmul(o, yT_hi[v][:, k, b, :], f_hi[:, k, :], start=(k == 0), stop=False)
                            pe.matmul(o, yT_hi[v][:, k, b, :], f_lo[:, k, :], start=False, stop=False)
                            last = pe.matmul(o, yT_lo[v][:, k, b, :], f_hi[:, k, :], start=False, stop=(k == KT - 1))
                    last.then_inc(f_done, 1)
                if is_pair(t - 2):
                    pe.wait_ge(yn_ready, t - 2 + 1)
                    wait_pairs(pe, out_ready, t - 2)
                    for k in range(KT):
                        for b in range(2):
                            at = (2 * k + b) * P
                            last = pe.transpose(bank_f[:, at:at + P], yn[:, w, b, k * P:(k + 1) * P], ident[:, :])
                    last.then_inc(yT_done, 1)

            run_periods(pe, period, 3, 1)


def flat(ap):
    ap = ap[:]
    names = " ".join("abcdef"[:len(ap.shape) - 1])
    return ap.rearrange(f"p {names} -> p ({names})") if len(ap.shape) > 2 else ap


def kernel(**inputs):
    import numpy as _np
    import concourse.bacc as _bacc
    from concourse import mybir as _mybir
    from concourse.bass_utils import run_bass_kernel_spmd as _run

    given = {n.removeprefix("L0_xattn_"): _np.asarray(a) for n, a in inputs.items()}
    norms = ("a_ln1", "a_ln2", "v_ln1", "v_ln2", "ln")
    vectors = [given[f"{n}_{k}"].reshape(-1, 128) for k in "gb" for n in norms]
    laid = {"x": given["x"], "ctx": given["ctx_512"], "fside": given["fside_BxSxS_0"]}
    for a in "av":
        for w in ("Wq", "Wk", "Wv", "Wo"):
            laid[f"{a}_{w}"] = given[f"{a}_{w}"]
    laid["fc_W"] = given["fc_W"]
    laid["norm_cols"] = _np.concatenate(vectors, axis=0).T
    laid["bias_rows"] = _np.stack([given[f"{a}_{b}"] for a in "av" for b in ("bq", "bk", "bv", "bo")]
                                  + [given["fc_b"]])[None]

    nc = _bacc.Bacc("TRN2", target_bir_lowering=False, num_devices=1)
    arrays, args = {}, []
    for name, a in laid.items():
        a = _np.ascontiguousarray(a)
        arrays[f"in_{name}"] = a
        args.append(nc.dram_tensor(f"in_{name}", a.shape, _mybir.dt.from_np(a.dtype), kind="ExternalInput").ap())
    shape = laid["x"].shape
    args.append(nc.dram_tensor("out_0", shape, _mybir.dt.from_np(laid["x"].dtype), kind="ExternalOutput").ap())
    xattn_kernel(nc, *args)
    r = _run(nc, [arrays], core_ids=[0])
    return r.results[0]["out_0"]
```

```python
import concourse.bass as bass
from concourse import mybir
from contextlib import ExitStack

FP32 = mybir.dt.float32
F32R = mybir.dt.float32r
ALU = mybir.AluOpType
ACT = mybir.ActivationFunctionType
AX = mybir.AxisListType

EPS = 1e-5
P = 128
WARM_UP = 24
RING = 4


def xattn_kernel(nc, x, ctx_in, fside, w_q, w_kv, w_o, fc_w, vector_cols, bias_rows, out):
    B, S, DT = x.shape
    E = w_q.shape[2]
    KT = DT // P
    KE = E // P
    PAIRS = B // 2
    SCALE = float(E) ** -0.5
    NORMS, BIASES = 8, 12
    LN1, LN2, LNF = (0, 3), (2, 5), 6
    BO, BFC = (0, 1), 2

    x_pairs = x.rearrange("(p b) s d -> p s b d", b=2)
    c_pairs = ctx_in.rearrange("(p b) s d -> p s b d", b=2)
    f_pairs = fside.rearrange("(p b) s d -> p s b d", b=2)
    out_pairs = out.rearrange("(p b) s d -> p s b d", b=2)

    es = ExitStack()
    with es:
        def sb(name, shape, dt=FP32):
            return es.enter_context(nc.sbuf_tensor(name, shape, dt))

        def pb(name):
            return es.enter_context(nc.psum_tensor(name, [P, 512], FP32))

        def sem(name):
            return es.enter_context(nc.semaphore(name))

        ident = sb("ident", [P, P])
        mean_dt = sb("mean_dt", [P, P])
        mean_dc = sb("mean_dc", [P, P])
        minus_half = sb("minus_half", [P, 6])
        eps = sb("eps", [P, 6])
        one = sb("one", [P, 6])
        cols = sb("cols", [P, 2 * NORMS + BIASES])
        shift_less_gain = sb("shift_less_gain", [P, NORMS])
        bias_cols = cols[:, 2 * NORMS:2 * NORMS + BIASES]
        rows = sb("rows", [1, 3, E])
        wq = sb("wq", [P, 2, KT, E])
        wkv = sb("wkv", [P, 2, 2, E])
        wo = sb("wo", [P, 2, KE, DT])
        wf = sb("wf", [P, KT, DT])
        gained_q = sb("gained_q", [P, 2, KT, E])
        gained_kv = sb("gained_kv", [P, 2, 2, E])
        row_sum = sb("row_sum", [P, BIASES])
        added_row = sb("added_row", [P, BIASES])
        scaled_f = sb("scaled_f", [P, KT, DT])
        f2 = sb("f2", [P, KT, DT])
        q2T = sb("q2T", [P, 2, KE, DT])
        k2T = sb("k2T", [P, 2, KE, P])
        v2T = sb("v2T", [P, 2, KE, P])
        m_hi = sb("m_hi", [P, 2, KT, P], F32R)
        m_lo = sb("m_lo", [P, 2, KT, P], F32R)
        o_hi = sb("o_hi", [P, 2, DT], F32R)
        o_lo = sb("o_lo", [P, 2, DT], F32R)
        f_hi = sb("f_hi", [P, KT, DT], F32R)
        f_lo = sb("f_lo", [P, KT, DT], F32R)

        x_all = sb("x_all", [P, PAIRS, 2, DT])
        raw = sb("raw", [P, RING, 2, 2, P])
        cn = sb("cn", [P, RING, 2, 2, P])
        y = sb("y", [P, RING, 2, DT])
        in_bn = sb("in_bn", [P, 2, 6, 6])
        in_mv = sb("in_mv", [P, 2, 6, 2])
        in_var_eps = sb("in_var_eps", [P, 2, 6])
        in_rstd = sb("in_rstd", [P, 2, 6])
        in_mean_rstd = sb("in_mean_rstd", [P, 2, 6])
        in_offset = sb("in_offset", [P, 2, 6])
        y_bn = sb("y_bn", [P, 2, 2, 6])
        y_mv = sb("y_mv", [P, 2, 2, 2])
        y_var_eps = sb("y_var_eps", [P, 2, 2])
        y_rstd = sb("y_rstd", [P, 2, 2])
        y_mean_rstd = sb("y_mean_rstd", [P, 2, 2])
        y_offset = sb("y_offset", [P, 2, 2])
        xn = sb("xn", [P, 2, 2, DT])
        xT_hi = [sb(f"xT_hi{s}", [P, KT, 2 * P], F32R) for s in range(2)]
        xT_lo = [sb(f"xT_lo{s}", [P, KT, 2 * P], F32R) for s in range(2)]
        cT = sb("cT", [P, 2, 2, 2, P])
        uT = sb("uT", [P, 2, 2, 2, P])
        neg_max = sb("neg_max", [P, 2, 4])
        exps = sb("exps", [P, 2, 4, P])
        exp_sum = sb("exp_sum", [P, 2, 4])
        inv_sum = sb("inv_sum", [P, 2, 4])
        attn = sb("attn", [P, 2, 4, P])
        attnT = sb("attnT", [P, 2, 4, P])
        acT_hi = [sb(f"acT_hi{s}", [P, 4, P], F32R) for s in range(2)]
        acT_lo = [sb(f"acT_lo{s}", [P, 4, P], F32R) for s in range(2)]
        yn = sb("yn", [P, 2, 2, DT])
        yT_hi = [sb(f"yT_hi{s}", [P, KT, 2, P], F32R) for s in range(2)]
        yT_lo = [sb(f"yT_lo{s}", [P, KT, 2, P], F32R) for s in range(2)]
        result = sb("result", [P, 2, 2, DT])

        bank_xT, bank_cT, bank_s, bank_pT = pb("bank_xT"), pb("bank_cT"), pb("bank_s"), pb("bank_pT")
        bank_ac, bank_u, bank_y, bank_f = pb("bank_ac"), pb("bank_u"), pb("bank_y"), pb("bank_f")

        ident_made, consts_made, half_made = sem("ident_made"), sem("consts_made"), sem("half_made")
        cols_in, rows_in = sem("cols_in"), sem("rows_in")
        wq_in, wkv_in, wo_in, wf_in = sem("wq_in"), sem("wkv_in"), sem("wo_in"), sem("wf_in")
        diff_made, q_gained, kv_gained = sem("diff_made"), sem("q_gained"), sem("kv_gained")
        sums_made, sums_biased, rows_made = sem("sums_made"), sem("sums_biased"), sem("rows_made")
        q_turned, k_turned, v_turned = sem("q_turned"), sem("k_turned"), sem("v_turned")
        q2T_made, k2T_made, v2T_made = sem("q2T_made"), sem("k2T_made"), sem("v2T_made")
        f_scaled, f_means_made, f_folded = sem("f_scaled"), sem("f_means_made"), sem("f_folded")
        m_made, o_made = sem("m_made"), sem("o_made")
        hi_made, lo_made = sem("hi_made"), sem("lo_made")

        loaded = [sem(f"loaded{s}") for s in range(RING)]
        stored = [sem(f"stored{s}") for s in range(2)]
        in_bn_done, in_mv_done = sem("in_bn_done"), sem("in_mv_done")
        in_var_done, in_rstd_done = sem("in_var_done"), sem("in_rstd_done")
        in_prod_done, in_norm_ready = sem("in_prod_done"), sem("in_norm_ready")
        y_bn_done, y_mv_done = sem("y_bn_done"), sem("y_mv_done")
        y_var_done, y_rstd_done = sem("y_var_done"), sem("y_rstd_done")
        y_prod_done, y_norm_ready = sem("y_prod_done"), sem("y_norm_ready")
        xn_ready, cn_ready, yn_ready = sem("xn_ready"), sem("cn_ready"), sem("yn_ready")
        xT_done, cT_done, s_done, pT_done = sem("xT_done"), sem("cT_done"), sem("s_done"), sem("pT_done")
        ac_done, u_done, y_done, yT_done, f_done = (sem(n) for n in (
            "ac_done", "u_done", "y_done", "yT_done", "f_done"))
        xhi_ready, xlo_ready, cT_ready, uT_ready = (sem(n) for n in (
            "xhi_ready", "xlo_ready", "cT_ready", "uT_ready"))
        max_ready, exp_ready, inv_ready, attn_ready = (sem(n) for n in (
            "max_ready", "exp_ready", "inv_ready", "attn_ready"))
        attnT_ready, achi_ready, aclo_ready = sem("attnT_ready"), sem("achi_ready"), sem("aclo_ready")
        y_ready, yhi_ready, ylo_ready, out_ready = (sem(n) for n in (
            "y_ready", "yhi_ready", "ylo_ready", "out_ready"))

        def is_pair(p):
            return not isinstance(p, int) or 0 <= p < PAIRS

        def wait_pairs(eng, semaphore, count):
            if not isinstance(count, int) or count > 0:
                eng.wait_ge(semaphore, count)

        def run_periods(eng, period, behind, ahead, skip=0, before={}):
            first = behind + skip
            rounds = (PAIRS - ahead - first) // RING
            after = first + rounds * RING
            for t in range(-ahead, first):
                before.get(t, lambda: None)()
                period(t, t)
            with eng.Fori(first, after - RING + 1, RING) as base:
                for j in range(RING):
                    period(base + j, first + j)
            for t in range(after, PAIRS + behind):
                period(t, t)

        q_banks, bank_k, bank_v, bank_sums = (bank_xT, bank_pT), bank_cT, bank_s, (bank_ac, bank_y)
        bank_m, bank_o, bank_fm = bank_u, bank_y, bank_f
        QK = 4 * KE

        def row_at(i, a, e):
            return (2 * i + a) * KE + e

        block = es.enter_context(nc.Block())

        @block.sync
        def _(sp):
            sp.dma_start(cols[:, :], vector_cols).then_inc(cols_in, 16)
            sp.dma_start(wq[:, :, :, :], w_q.rearrange("a (k p) e -> p a k e", p=P)).then_inc(wq_in, 16)
            sp.dma_start(wkv[:, :, :, :], w_kv.rearrange("a i p e -> p a i e")).then_inc(wkv_in, 16)

            def load(p, s):
                wait_pairs(sp, cn_ready, p - RING + 1)
                arrived = loaded[s % RING]
                sp.dma_start(x_all[:, bass.ds(p, 1), :, :], x_pairs[bass.ds(p, 1)].rearrange("p s b d -> s p b d")).then_inc(arrived, 16)
                sp.dma_start(raw[:, s % RING, 0, :, :], c_pairs[bass.ds(p, 1)].rearrange("p s b d -> s (p b) d")).then_inc(arrived, 16)
                sp.dma_start(raw[:, s % RING, 1, :, :], f_pairs[bass.ds(p, 1)].rearrange("p s b d -> s (p b) d")).then_inc(arrived, 16)

            def period(t, s):
                if is_pair(t - 4):
                    sp.wait_ge(out_ready, t - 4 + 1)
                    sp.dma_start(out_pairs[bass.ds(t - 4, 1)].rearrange("p s b d -> s (p b) d"),
                                 result[:, s % 2, :, :]).then_inc(stored[s % 2], 16)
                if is_pair(t + 5):
                    load(t + 5, s + 5)


            def load_wo():
                sp.dma_start(wo[:, :, :, :], w_o.rearrange("a (k p) d -> p a k d", p=P)).then_inc(wo_in, 16)

            def load_wf():
                sp.dma_start(rows[:, :, :], bias_rows).then_inc(rows_in, 16)
                sp.dma_start(wf[:, :, :], fc_w.rearrange("(k p) d -> p k d", p=P)).then_inc(wf_in, 16)

            run_periods(sp, period, 4, 5, before={-3: load_wf, -2: load_wo})
            for s in range(2):
                sp.wait_ge(stored[s], 16 * (PAIRS // 2))

        @block.gpsimd
        def _(pool):
            pool.memset(ident[:, :], 0.0).then_inc(ident_made, 1)
            pool.memset(eps[:, :], EPS)
            pool.memset(one[:, :], 1.0)
            pool.memset(minus_half[:, :], -0.5).then_inc(half_made, 1)
            pool.wait_ge(ident_made, 1)
            pool.affine_select(out=ident[:, :], in_=ident[:, :], compare_op=ALU.not_equal, fill=1.0,
                               base=0, pattern=[[-1, P]], channel_multiplier=1).then_inc(ident_made, 1)

            def norm_scalars(p, mv, mv_done, var_eps, var_done, rstd, rstd_done, prod, prod_done, offset, ready):
                pool.wait_ge(mv_done, p + 1)
                rows = var_eps.shape[1]
                pool.tensor_tensor(var_eps, mv[:, :, 1], eps[:, 0:rows], ALU.add).then_inc(var_done, 1)
                pool.wait_ge(var_done, p + 1)
                pool.tensor_tensor(rstd, var_eps, minus_half[:, 0:rows], ALU.pow).then_inc(rstd_done, 1)
                pool.wait_ge(rstd_done, p + 1)
                pool.tensor_tensor(prod, mv[:, :, 0], rstd, ALU.mult).then_inc(prod_done, 1)
                pool.wait_ge(prod_done, p + 1)
                pool.tensor_tensor(offset, one[:, 0:rows], prod, ALU.subtract).then_inc(ready, 1)

            pool.wait_ge(half_made, 1)

            def period(t, s):
                if is_pair(t + 2):
                    p, w = t + 2, s % 2
                    wait_pairs(pool, xn_ready, p - 1)
                    norm_scalars(p, in_mv[:, w], in_mv_done, in_var_eps[:, w], in_var_done, in_rstd[:, w],
                                 in_rstd_done, in_mean_rstd[:, w], in_prod_done, in_offset[:, w], in_norm_ready)
                    pool.wait_ge(in_norm_ready, p + 1)
                    wait_pairs(pool, ac_done, p - 3)
                if is_pair(t - 2):
                    w = s % 2
                    norm_scalars(t - 2, y_mv[:, w], y_mv_done, y_var_eps[:, w], y_var_done, y_rstd[:, w],
                                 y_rstd_done, y_mean_rstd[:, w], y_prod_done, y_offset[:, w], y_norm_ready)
                if is_pair(t + 2):
                    w, r = s % 2, (s + 2) % RING
                    for a in range(2):
                        for b in range(2):
                            i = 2 + 2 * a + b
                            last = pool.tensor_scalar(cn[:, r, a, b, :], raw[:, r, a, b, :], in_rstd[:, w, i:i + 1],
                                                      in_offset[:, w, i:i + 1], ALU.mult, ALU.add)
                    last.then_inc(cn_ready, 1)
                if is_pair(t):
                    w = s % 2
                    pool.wait_ge(inv_ready, t + 1)
                    wait_pairs(pool, pT_done, t - 1)
                    pool.tensor_tensor(attn[:, w], exps[:, w], inv_sum[:, w].unsqueeze(2).to_broadcast([P, 4, P]),
                                       ALU.mult).then_inc(attn_ready, 1)

            run_periods(pool, period, 2, 2)

        @block.scalar
        def _(act):
            def make_q2T():
                act.wait_ge(rows_made, 1)
                for a in range(2):
                    act.wait_ge(q_turned, a + 1)
                    for e in range(KE):
                        act.activation(q2T[:, a, e, :], q_banks[a][:, e * DT:(e + 1) * DT], ACT.Identity,
                                       bias=added_row[:, row_at(0, a, e):row_at(0, a, e) + 1]).then_inc(q2T_made, 1)

            def make_v2T():
                act.wait_ge(rows_made, 2)
                act.wait_ge(v_turned, 1)
                for a in range(2):
                    for e in range(KE):
                        at = (a * KE + e) * P
                        act.activation(v2T[:, a, e, :], bank_v[:, at:at + P], ACT.Identity,
                                       bias=added_row[:, row_at(2, a, e):row_at(2, a, e) + 1]).then_inc(v2T_made, 1)

            def make_m_hi():
                act.wait_ge(m_made, 1)
                act.activation(flat(m_hi), bank_m[:, :], ACT.Copy, scale=SCALE).then_inc(hi_made, 1)

            def make_o_f_hi():
                act.wait_ge(o_made, 1)
                act.activation(flat(o_hi), bank_o[:, :], ACT.Copy).then_inc(hi_made, 1)
                act.wait_ge(f_folded, 1)
                act.activation(flat(f_hi), flat(f2), ACT.Copy).then_inc(hi_made, 1)

            def make_v2T_m_hi():
                make_v2T()
                make_m_hi()

            make_q2T()

            def period(t, s):
                w, v = s % 2, (s + 1) % 2
                if is_pair(t - 3):
                    act.wait_ge(yT_done, t - 3 + 1)
                    act.activation(flat(yT_hi[v]), bank_ac[:, :], ACT.Copy).then_inc(yhi_ready, 1)
                if is_pair(t + 1):
                    act.wait_ge(xT_done, t + 1 + 1)
                    wait_pairs(act, u_done, t + 1 - 1)
                    act.activation(flat(xT_hi[v]), bank_xT[:, :], ACT.Copy).then_inc(xhi_ready, 1)
                if is_pair(t - 1):
                    act.wait_ge(pT_done, t - 1 + 1)
                    wait_pairs(act, ac_done, t - 1 - 1)
                    act.activation(flat(attnT[:, v]), bank_pT[:, :], ACT.Copy).then_inc(attnT_ready, 1)
                if is_pair(t + 1):
                    act.wait_ge(cT_done, t + 1 + 1)
                    wait_pairs(act, s_done, t + 1 - 1)
                    act.activation(flat(cT[:, v]), bank_cT[:, :], ACT.Copy).then_inc(cT_ready, 1)
                if is_pair(t + 2):
                    act.wait_ge(in_norm_ready, t + 2 + 1)
                    wait_pairs(act, xT_done, t + 2 - 1)
                    for b in range(2):
                        last = act.activation(xn[:, w, b, :], x_all[:, bass.ds(t + 2, 1), b, :], ACT.Identity,
                                              bias=in_offset[:, w, b:b + 1], scale=in_rstd[:, w, b:b + 1])
                    last.then_inc(xn_ready, 1)
                if is_pair(t - 1):
                    act.wait_ge(ac_done, t - 1 + 1)
                    wait_pairs(act, y_done, t - 1 - 1)
                    act.activation(flat(acT_hi[v]), bank_ac[:, :], ACT.Copy).then_inc(achi_ready, 1)
                if is_pair(t):
                    act.wait_ge(max_ready, t + 1)
                    wait_pairs(act, attn_ready, t - 1)
                    for i in range(4):
                        last = act.activation(exps[:, w, i, :], bank_s[:, i * P:(i + 1) * P], ACT.Exp,
                                              bias=neg_max[:, w, i:i + 1], accum_out=exp_sum[:, w, i:i + 1])
                    last.then_inc(exp_ready, 1)
                if is_pair(t + 1):
                    act.wait_ge(u_done, t + 1 + 1)
                    wait_pairs(act, s_done, t + 1 - 1)
                    act.activation(flat(uT[:, v]), bank_u[:, :], ACT.Copy).then_inc(uT_ready, 1)
                if is_pair(t - 2):
                    act.wait_ge(y_norm_ready, t - 2 + 1)
                    for b in range(2):
                        last = act.activation(yn[:, w, b, :], y[:, (s - 2) % RING, b, :], ACT.Identity,
                                              bias=y_offset[:, w, b:b + 1], scale=y_rstd[:, w, b:b + 1])
                    last.then_inc(yn_ready, 1)

            run_periods(act, period, 3, 2, before={-1: make_v2T_m_hi, 1: make_o_f_hi})

        @block.vector
        def _(dve):
            dve.memset(mean_dt[:, :], 1.0 / DT)
            dve.memset(mean_dc[:, :], 1.0 / P).then_inc(consts_made, 1)
            dve.wait_ge(cols_in, 16)
            dve.tensor_tensor(shift_less_gain[:, :], cols[:, NORMS:2 * NORMS], cols[:, 0:NORMS],
                              ALU.subtract).then_inc(diff_made, 1)

            def added_rows(n, cs, parts):
                dve.wait_ge(sums_made, n)
                dve.tensor_tensor(row_sum[:, cs], bank_sums[n - 1][:, cs], bias_cols[:, cs], ALU.add).then_inc(sums_biased, 1)
                dve.wait_ge(sums_biased, n)
                for lo, hi, width in parts:
                    last = dve.tensor_scalar(added_row[:, lo:hi], row_sum[:, lo:hi], 1.0 / width, None, ALU.mult)
                last.then_inc(rows_made, 1)

            dve.wait_ge(wq_in, 16)
            for a in range(2):
                for k in range(KT):
                    last = dve.tensor_scalar(gained_q[:, a, k, :], wq[:, a, k, :],
                                             cols[:, LN1[a] + k:LN1[a] + k + 1], None, ALU.mult)
                last.then_inc(q_gained, 1)
            dve.wait_ge(wkv_in, 16)
            for a in range(2):
                last = dve.tensor_scalar(gained_kv[:, a], wkv[:, a], cols[:, LN2[a]:LN2[a] + 1], None, ALU.mult)
            last.then_inc(kv_gained, 1)

            def make_k2T():
                added_rows(1, slice(0, QK), ((0, QK // 2, DT), (QK // 2, QK, P)))
                dve.wait_ge(rows_made, 1)
                dve.wait_ge(k_turned, 1)
                for a in range(2):
                    for e in range(KE):
                        at = (a * KE + e) * P
                        last = dve.tensor_scalar(k2T[:, a, e, :], bank_k[:, at:at + P],
                                                 added_row[:, row_at(1, a, e):row_at(1, a, e) + 1], None, ALU.add)
                last.then_inc(k2T_made, 1)
                added_rows(2, slice(QK, BIASES), ((QK, BIASES, P),))

            def scale_f_make_m_lo():
                dve.wait_ge(wf_in, 16)
                for k in range(KT):
                    last = dve.tensor_scalar(scaled_f[:, k, :], wf[:, k, :],
                                             shift_less_gain[:, LNF + k:LNF + k + 1], None, ALU.mult)
                last.then_inc(f_scaled, 1)
                dve.wait_ge(hi_made, 1)
                dve.scalar_tensor_tensor(flat(m_lo), bank_m[:, :], SCALE, flat(m_hi).bitcast(FP32),
                                         ALU.mult, ALU.subtract).then_inc(lo_made, 1)

            def fold_f():
                dve.wait_ge(f_means_made, 1)
                for k in range(KT):
                    last = dve.scalar_tensor_tensor(f2[:, k, :], wf[:, k, :], cols[:, LNF + k:LNF + k + 1],
                                                    bank_fm[:, 0:DT], ALU.mult, ALU.add)
                last.then_inc(f_folded, 1)

            def make_o_f_lo():
                dve.wait_ge(hi_made, 2)
                dve.tensor_tensor(flat(o_lo), bank_o[:, :], flat(o_hi).bitcast(FP32), ALU.subtract).then_inc(lo_made, 1)
                dve.wait_ge(hi_made, 3)
                dve.tensor_tensor(flat(f_lo), flat(f2), flat(f_hi).bitcast(FP32), ALU.subtract).then_inc(lo_made, 1)

            def period(t, s):
                w, v, r = s % 2, (s + 1) % 2, s % RING
                if is_pair(t - 2):
                    dve.wait_ge(y_bn_done, t - 2 + 1)
                    wait_pairs(dve, y_norm_ready, t - 2 - 1)
                if is_pair(t - 4):
                    p = t - 4
                    dve.wait_ge(f_done, p + 1)
                    wait_pairs(dve, stored[w], 8 * (p - w))
                    dve.tensor_tensor(flat(result[:, w]), bank_f[:, :], flat(y[:, r]), ALU.add).then_inc(out_ready, 1)
                if is_pair(t - 2):
                    for b in range(2):
                        last = dve.bn_aggr(y_mv[:, w, b, :], y_bn[:, w, b, :])
                    last.then_inc(y_mv_done, 1)
                if is_pair(t - 3):
                    dve.wait_ge(yhi_ready, t - 3 + 1)
                    dve.tensor_tensor(flat(yT_lo[v]), bank_ac[:, :], flat(yT_hi[v]).bitcast(FP32),
                                      ALU.subtract).then_inc(ylo_ready, 1)
                if is_pair(t + 1):
                    dve.wait_ge(xhi_ready, t + 1 + 1)
                    dve.tensor_tensor(flat(xT_lo[v]), bank_xT[:, :], flat(xT_hi[v]).bitcast(FP32),
                                      ALU.subtract).then_inc(xlo_ready, 1)
                if is_pair(t):
                    dve.wait_ge(s_done, t + 1)
                    wait_pairs(dve, exp_ready, t - 1)
                    dve.tensor_reduce(neg_max[:, w], bank_s[:, :].rearrange("p (i k) -> p i k", i=4), AX.X, ALU.max,
                                      negate=True).then_inc(max_ready, 1)
                if is_pair(t + 3):
                    dve.wait_ge(loaded[(s + 3) % RING], 12 * (t + 3 - (s + 3) % RING) + 48)
                    for b in range(2):
                        dve.bn_stats(in_bn[:, v, b, :], x_all[:, bass.ds(t + 3, 1), b, :])
                if is_pair(t - 1):
                    dve.wait_ge(achi_ready, t - 1 + 1)
                    dve.tensor_tensor(flat(acT_lo[v]), bank_ac[:, :], flat(acT_hi[v]).bitcast(FP32),
                                      ALU.subtract).then_inc(aclo_ready, 1)
                if is_pair(t + 3):
                    for i in range(4):
                        last = dve.bn_stats(in_bn[:, v, 2 + i, :], raw[:, (s + 3) % RING, i // 2, i % 2, :])
                    last.then_inc(in_bn_done, 1)
                    wait_pairs(dve, in_norm_ready, t + 3 - 1)
                    dve.wait_ge(in_bn_done, t + 3 + 1)
                if is_pair(t):
                    dve.wait_ge(exp_ready, t + 1)
                    wait_pairs(dve, attn_ready, t - 1)
                    dve.reciprocal(inv_sum[:, w], exp_sum[:, w]).then_inc(inv_ready, 1)
                if is_pair(t + 3):
                    for i in range(6):
                        last = dve.bn_aggr(in_mv[:, v, i, :], in_bn[:, v, i, :])
                    last.then_inc(in_mv_done, 1)
                if is_pair(t - 1):
                    p = t - 1
                    dve.wait_ge(y_done, p + 1)
                    dve.tensor_tensor(y[:, (s - 1) % RING], bank_y[:, :].rearrange("p (b d) -> p b d", b=2),
                                      x_all[:, bass.ds(p, 1), :, :].rearrange("p o b d -> p (o b) d"),
                                      ALU.add).then_inc(y_ready, 1)
                    dve.wait_ge(y_ready, p + 1)
                    for b in range(2):
                        last = dve.bn_stats(y_bn[:, v, b, :], y[:, (s - 1) % RING, b, :])
                    last.then_inc(y_bn_done, 1)

            run_periods(dve, period, 4, 3, skip=2, before={-2: make_k2T, -1: scale_f_make_m_lo, 0: fold_f, 1: make_o_f_lo})

        @block.tensor
        def _(pe):
            pe.wait_ge(ident_made, 2)
            for _ in range(WARM_UP):
                pe.transpose(bank_f[:, 0:P], ident[:, :], ident[:, :])
            pe.wait_ge(diff_made, 1)
            pe.wait_ge(wq_in, 16)
            for a in range(2):
                for e in range(KE):
                    at = row_at(0, a, e)
                    for k in range(KT):
                        pe.matmul(bank_sums[0][:, at:at + 1], wq[:, a, k, e * P:(e + 1) * P],
                                  shift_less_gain[:, LN1[a] + k:LN1[a] + k + 1], start=(k == 0), stop=(k == KT - 1))
            for a in range(2):
                pe.wait_ge(q_gained, a + 1)
                for e in range(KE):
                    for k in range(KT):
                        at = (e * KT + k) * P
                        last = pe.transpose(q_banks[a][:, at:at + P], gained_q[:, a, k, e * P:(e + 1) * P], ident[:, :])
                last.then_inc(q_turned, 1)
            pe.wait_ge(wkv_in, 16)
            pe.wait_ge(kv_gained, 1)
            for i, (bank, done) in enumerate(((bank_k, k_turned), (bank_v, v_turned))):
                for a in range(2):
                    for e in range(KE):
                        at = row_at(1 + i, a, e)
                        last = pe.matmul(bank_sums[i][:, at:at + 1], wkv[:, a, i, e * P:(e + 1) * P],
                                         shift_less_gain[:, LN2[a]:LN2[a] + 1], start=True, stop=True)
                last.then_inc(sums_made, 1)
                for a in range(2):
                    for e in range(KE):
                        at = (a * KE + e) * P
                        last = pe.transpose(bank[:, at:at + P], gained_kv[:, a, i, e * P:(e + 1) * P], ident[:, :])
                last.then_inc(done, 1)
            pe.wait_ge(k2T_made, 1)
            for a in range(2):
                pe.wait_ge(q2T_made, KE * (a + 1))
                for k in range(KT):
                    at = (a * KT + k) * P
                    for e in range(KE):
                        last = pe.matmul(bank_m[:, at:at + P], q2T[:, a, e, k * P:(k + 1) * P], k2T[:, a, e, :],
                                         start=(e == 0), stop=(e == KE - 1))
            last.then_inc(m_made, 1)

            def make_f_means():
                pe.wait_ge(consts_made, 1)
                pe.wait_ge(rows_in, 16)
                pe.wait_ge(f_scaled, 1)
                for k in range(KT):
                    pe.matmul(bank_fm[:, 0:DT], mean_dt[:, :], scaled_f[:, k, :], start=(k == 0), stop=False)
                pe.matmul(bank_fm[:, 0:DT], mean_dt[0:1, :], rows[0:1, BFC, :], start=False,
                          stop=True).then_inc(f_means_made, 1)

            def make_o():
                pe.wait_ge(wo_in, 16)
                pe.wait_ge(v2T_made, 2 * KE)
                for a in range(2):
                    o = bank_o[:, a * DT:(a + 1) * DT]
                    for e in range(KE):
                        pe.matmul(o, v2T[:, a, e, :], wo[:, a, e, :], start=(e == 0), stop=False)
                    last = pe.matmul(o, mean_dc[0:1, :], rows[0:1, BO[a], :], start=False, stop=True)
                last.then_inc(o_made, 1)

            def period(t, s):
                w, v = s % 2, (s + 1) % 2
                if is_pair(t + 1):
                    p = t + 1
                    pe.wait_ge(xn_ready, p + 1)
                    wait_pairs(pe, xlo_ready, p)
                    for k in range(KT):
                        for b in range(2):
                            at = (2 * k + b) * P
                            last = pe.transpose(bank_xT[:, at:at + P], xn[:, v, b, k * P:(k + 1) * P], ident[:, :])
                    last.then_inc(xT_done, 1)
                if is_pair(t - 1):
                    pe.wait_ge(attn_ready, t - 1 + 1)
                    wait_pairs(pe, attnT_ready, t - 1)
                    for i in range(4):
                        last = pe.transpose(bank_pT[:, i * P:(i + 1) * P], attn[:, v, i, :], ident[:, :])
                    last.then_inc(pT_done, 1)
                if isinstance(t, int) and t == -1:
                    make_f_means()
                if is_pair(t + 1):
                    p, r = t + 1, (s + 1) % RING
                    pe.wait_ge(cn_ready, p + 1)
                    wait_pairs(pe, cT_ready, p)
                    for a in range(2):
                        for b in range(2):
                            at = (2 * a + b) * P
                            last = pe.transpose(bank_cT[:, at:at + P], cn[:, r, a, b, :], ident[:, :])
                    last.then_inc(cT_done, 1)
                if is_pair(t):
                    pe.wait_ge(cT_ready, t + 1)
                    pe.wait_ge(uT_ready, t + 1)
                    if isinstance(t, int) and t == 0:
                        pe.wait_ge(v2T_made, 2 * KE)
                    wait_pairs(pe, exp_ready, t)
                    for a in range(2):
                        for b in range(2):
                            at = (2 * a + b) * P
                            last = pe.matmul(bank_s[:, at:at + P], uT[:, w, a, b, :], cT[:, w, a, b, :],
                                             start=True, stop=True)
                    last.then_inc(s_done, 1)
                if is_pair(t - 1):
                    pe.wait_ge(attnT_ready, t - 1 + 1)
                    wait_pairs(pe, ylo_ready, t - 2)
                    for i in range(4):
                        last = pe.matmul(bank_ac[:, i * P:(i + 1) * P], cn[:, (s - 1) % RING, i // 2, i % 2, :],
                                         attnT[:, v, i, :], start=True, stop=True)
                    last.then_inc(ac_done, 1)
                if isinstance(t, int) and t == -1:
                    pe.wait_ge(lo_made, 1)
                if is_pair(t + 1):
                    pe.wait_ge(xhi_ready, t + 1 + 1)
                    wait_pairs(pe, uT_ready, t + 1)
                    for a in range(2):
                        u = bank_u[:, a * 2 * P:(a + 1) * 2 * P]
                        for k in range(KT):
                            pe.matmul(u, m_hi[:, a, k, :], xT_hi[v][:, k, :], start=(k == 0), stop=False)
                            pe.matmul(u, m_lo[:, a, k, :], xT_hi[v][:, k, :], start=False, stop=False)
                        if a == 0:
                            pe.wait_ge(xlo_ready, t + 1 + 1)
                        for k in range(KT):
                            last = pe.matmul(u, m_hi[:, a, k, :], xT_lo[v][:, k, :], start=False, stop=(k == KT - 1))
                    last.then_inc(u_done, 1)
                if isinstance(t, int) and t == 1:
                    pe.wait_ge(lo_made, 3)
                if is_pair(t - 1):
                    pe.wait_ge(achi_ready, t - 1 + 1)
                    wait_pairs(pe, y_ready, t - 1)
                    for b in range(2):
                        o = bank_y[:, b * DT:(b + 1) * DT]
                        for a in range(2):
                            pe.matmul(o, acT_hi[v][:, 2 * a + b, :], o_hi[:, a, :], start=(a == 0), stop=False)
                            pe.matmul(o, acT_hi[v][:, 2 * a + b, :], o_lo[:, a, :], start=False, stop=False)
                        if b == 0:
                            pe.wait_ge(aclo_ready, t - 1 + 1)
                        for a in range(2):
                            last = pe.matmul(o, acT_lo[v][:, 2 * a + b, :], o_hi[:, a, :], start=False, stop=(a == 1))
                    last.then_inc(y_done, 1)
                if is_pair(t - 3):
                    pe.wait_ge(ylo_ready, t - 3 + 1)
                    wait_pairs(pe, out_ready, t - 3)
                    for b in range(2):
                        o = bank_f[:, b * DT:(b + 1) * DT]
                        for k in range(KT):
                            pe.matmul(o, yT_hi[v][:, k, b, :], f_hi[:, k, :], start=(k == 0), stop=False)
                            pe.matmul(o, yT_hi[v][:, k, b, :], f_lo[:, k, :], start=False, stop=False)
                            last = pe.matmul(o, yT_lo[v][:, k, b, :], f_hi[:, k, :], start=False, stop=(k == KT - 1))
                    last.then_inc(f_done, 1)
                if is_pair(t - 2):
                    pe.wait_ge(yn_ready, t - 2 + 1)
                    wait_pairs(pe, aclo_ready, min(t, PAIRS) if isinstance(t, int) else t)
                    for k in range(KT):
                        for b in range(2):
                            at = (2 * k + b) * P
                            last = pe.transpose(bank_ac[:, at:at + P], yn[:, w, b, k * P:(k + 1) * P], ident[:, :])
                    last.then_inc(yT_done, 1)

            run_periods(pe, period, 3, 1, skip=1, before={0: make_o})


def flat(ap):
    ap = ap[:]
    names = " ".join("abcdef"[:len(ap.shape) - 1])
    return ap.rearrange(f"p {names} -> p ({names})") if len(ap.shape) > 2 else ap


def kernel(**inputs):
    import numpy as _np
    import concourse.bacc as _bacc
    from concourse import mybir as _mybir
    from concourse.bass_utils import run_bass_kernel_spmd as _run

    given = {n.removeprefix("L0_xattn_"): _np.asarray(a) for n, a in inputs.items()}
    norms = ("a_ln1", "a_ln2", "v_ln1", "v_ln2", "ln")
    vectors = [given[f"{n}_{k}"].reshape(-1, 128) for k in "gb" for n in norms]
    vectors += [given[f"{a}_{b}"].reshape(-1, 128) for b in ("bq", "bk", "bv") for a in "av"]
    laid = {
        "x": given["x"], "ctx": given["ctx_512"], "fside": given["fside_BxSxS_0"],
        "Wq": _np.stack([given[f"{a}_Wq"] for a in "av"]),
        "Wkv": _np.stack([_np.stack([given[f"{a}_Wk"], given[f"{a}_Wv"]]) for a in "av"]),
        "Wo": _np.stack([given[f"{a}_Wo"] for a in "av"]),
        "fc_W": given["fc_W"],
        "vector_cols": _np.concatenate(vectors, axis=0).T,
        "bias_rows": _np.stack([given["a_bo"], given["v_bo"], given["fc_b"]])[None],
    }

    nc = _bacc.Bacc("TRN2", target_bir_lowering=False, num_devices=1)
    arrays, args = {}, []
    for name, a in laid.items():
        a = _np.ascontiguousarray(a)
        arrays[f"in_{name}"] = a
        args.append(nc.dram_tensor(f"in_{name}", a.shape, _mybir.dt.from_np(a.dtype), kind="ExternalInput").ap())
    shape = laid["x"].shape
    args.append(nc.dram_tensor("out_0", shape, _mybir.dt.from_np(laid["x"].dtype), kind="ExternalOutput").ap())
    xattn_kernel(nc, *args)
    r = _run(nc, [arrays], core_ids=[0])
    return r.results[0]["out_0"]
```

```python
import concourse.bass as bass
from concourse import mybir
from contextlib import ExitStack

FP32 = mybir.dt.float32
F32R = mybir.dt.float32r
ALU = mybir.AluOpType
ACT = mybir.ActivationFunctionType
AX = mybir.AxisListType

EPS = 1e-5
P = 128
WARM_UP = 12
RING = 4


def xattn_kernel(nc, x, ctx_in, fside, w_q, w_kv, w_o, fc_w, vector_cols, bias_rows, out):
    B, S, DT = x.shape
    E = w_q.shape[2]
    KT = DT // P
    KE = E // P
    PAIRS = B // 2
    SCALE = float(E) ** -0.5
    NORMS, BIASES = 8, 12
    LN1, LN2, LNF = (0, 3), (2, 5), 6
    BO, BFC = (0, 1), 2

    x_pairs = x.rearrange("(p b) s d -> p s b d", b=2)
    c_pairs = ctx_in.rearrange("(p b) s d -> p s b d", b=2)
    f_pairs = fside.rearrange("(p b) s d -> p s b d", b=2)
    out_pairs = out.rearrange("(p b) s d -> p s b d", b=2)

    es = ExitStack()
    with es:
        def sb(name, shape, dt=FP32):
            return es.enter_context(nc.sbuf_tensor(name, shape, dt))

        def pb(name):
            return es.enter_context(nc.psum_tensor(name, [P, 512], FP32))

        def sem(name):
            return es.enter_context(nc.semaphore(name))

        ident = sb("ident", [P, P])
        mean_dt = sb("mean_dt", [P, P])
        mean_dc = sb("mean_dc", [P, P])
        minus_half = sb("minus_half", [P, 6])
        eps = sb("eps", [P, 6])
        one = sb("one", [P, 6])
        cols = sb("cols", [P, 2 * NORMS + BIASES])
        shift_less_gain = sb("shift_less_gain", [P, NORMS])
        bias_cols = cols[:, 2 * NORMS:2 * NORMS + BIASES]
        rows = sb("rows", [1, 3, E])
        wq = sb("wq", [P, 2, KT, E])
        wkv = sb("wkv", [P, 2, 2, E])
        wo = sb("wo", [P, 2, KE, DT])
        wf = sb("wf", [P, KT, DT])
        turn_q = sb("turn_q", [P, 2, KT, P + 1])
        share_kv = sb("share_kv", [P, 2])
        turn_kv = sb("turn_kv", [P, 2, P])
        first_exp = sb("first_exp", [P, 1])
        bias_share = sb("bias_share", [P, BIASES])
        half_q = sb("half_q", [P, 2, KE])
        added_q = sb("added_q", [P, 2, KE])
        scaled_f = sb("scaled_f", [P, KT, DT])
        f2 = sb("f2", [P, KT, DT])
        q2T = sb("q2T", [P, 2, KE, DT])
        k2T = sb("k2T", [P, 2, KE, P])
        v2T = sb("v2T", [P, 2, KE, P])
        m_hi = sb("m_hi", [P, 2, KT, P], F32R)
        m_lo = sb("m_lo", [P, 2, KT, P], F32R)
        o_hi = sb("o_hi", [P, 2, DT], F32R)
        o_lo = sb("o_lo", [P, 2, DT], F32R)
        f_hi = sb("f_hi", [P, KT, DT], F32R)
        f_lo = sb("f_lo", [P, KT, DT], F32R)

        x_all = sb("x_all", [P, PAIRS, 2, DT])
        raw = sb("raw", [P, RING, 2, 2, P])
        cn = sb("cn", [P, RING, 2, 2, P])
        y = sb("y", [P, RING, 2, DT])
        in_bn = sb("in_bn", [P, 2, 6, 6])
        in_mv = sb("in_mv", [P, 2, 6, 2])
        in_var_eps = sb("in_var_eps", [P, 2, 6])
        in_rstd = sb("in_rstd", [P, 2, 6])
        in_mean_rstd = sb("in_mean_rstd", [P, 2, 6])
        in_offset = sb("in_offset", [P, 2, 6])
        y_bn = sb("y_bn", [P, 2, 2, 6])
        y_mv = sb("y_mv", [P, 2, 2, 2])
        y_var_eps = sb("y_var_eps", [P, 2, 2])
        y_rstd = sb("y_rstd", [P, 2, 2])
        y_mean_rstd = sb("y_mean_rstd", [P, 2, 2])
        y_offset = sb("y_offset", [P, 2, 2])
        xn = sb("xn", [P, 2, 2, DT])
        xT_hi = [sb(f"xT_hi{s}", [P, KT, 2 * P], F32R) for s in range(2)]
        xT_lo = [sb(f"xT_lo{s}", [P, KT, 2 * P], F32R) for s in range(2)]
        cT = sb("cT", [P, 2, 2, 2, P])
        uT = sb("uT", [P, 2, 2, 2, P])
        neg_max = sb("neg_max", [P, 2, 4])
        exps = sb("exps", [P, 2, 4, P])
        exp_sum = sb("exp_sum", [P, 2, 4])
        inv_sum = sb("inv_sum", [P, 2, 4])
        attn = sb("attn", [P, 2, 4, P])
        attnT = sb("attnT", [P, 2, 4, P])
        acT_hi = [sb(f"acT_hi{s}", [P, 4, P], F32R) for s in range(2)]
        acT_lo = [sb(f"acT_lo{s}", [P, 4, P], F32R) for s in range(2)]
        yn = sb("yn", [P, 2, 2, DT])
        yT_hi = [sb(f"yT_hi{s}", [P, KT, 2, P], F32R) for s in range(2)]
        yT_lo = [sb(f"yT_lo{s}", [P, KT, 2, P], F32R) for s in range(2)]
        result = sb("result", [P, 2, 2, DT])

        bank_xT, bank_cT, bank_s, bank_pT = pb("bank_xT"), pb("bank_cT"), pb("bank_s"), pb("bank_pT")
        bank_ac, bank_u, bank_y, bank_f = pb("bank_ac"), pb("bank_u"), pb("bank_y"), pb("bank_f")

        ident_made, consts_made, half_made = sem("ident_made"), sem("consts_made"), sem("half_made")
        cols_in, rows_in = sem("cols_in"), sem("rows_in")
        wq_in = [sem(f"wq_in{a}") for a in range(2)]
        wkv_in = [sem("wk_in"), sem("wv_in")]
        wo_in, wf_in = sem("wo_in"), sem("wf_in")
        diff_made, share_made = sem("diff_made"), sem("share_made")
        turn_q_made, turn_kv_made = sem("turn_q_made"), sem("turn_kv_made")
        half_q_made, added_q_made = sem("half_q_made"), sem("added_q_made")
        q_turned, k_turned, v_turned = sem("q_turned"), sem("k_turned"), sem("v_turned")
        q2T_made, k2T_made, v2T_made = sem("q2T_made"), sem("k2T_made"), sem("v2T_made")
        f_scaled, f_means_made, f_folded = sem("f_scaled"), sem("f_means_made"), sem("f_folded")
        m_made, o_made = sem("m_made"), sem("o_made")
        hi_made, lo_made = sem("hi_made"), sem("lo_made")

        loaded = [sem(f"loaded{s}") for s in range(RING)]
        stored = [sem(f"stored{s}") for s in range(2)]
        y_first_done, yn_second_ready = sem("y_first_done"), sem("yn_second_ready")
        f_first_done, out_first_ready = sem("f_first_done"), sem("out_first_ready")
        in_bn_done, in_mv_done = sem("in_bn_done"), sem("in_mv_done")
        in_var_done, in_rstd_done = sem("in_var_done"), sem("in_rstd_done")
        in_prod_done, in_norm_ready = sem("in_prod_done"), sem("in_norm_ready")
        y_bn_done, y_mv_done = sem("y_bn_done"), sem("y_mv_done")
        y_var_done, y_rstd_done = sem("y_var_done"), sem("y_rstd_done")
        y_prod_done, y_norm_ready = sem("y_prod_done"), sem("y_norm_ready")
        xn_ready, cn_ready, yn_ready = sem("xn_ready"), sem("cn_ready"), sem("yn_ready")
        xT_done, cT_done, s_done, pT_done = sem("xT_done"), sem("cT_done"), sem("s_done"), sem("pT_done")
        ac_done, u_done, y_done, yT_done, f_done = (sem(n) for n in (
            "ac_done", "u_done", "y_done", "yT_done", "f_done"))
        xhi_ready, xlo_ready, cT_ready, uT_ready = (sem(n) for n in (
            "xhi_ready", "xlo_ready", "cT_ready", "uT_ready"))
        max_ready, exp_ready, inv_ready, attn_ready = (sem(n) for n in (
            "max_ready", "exp_ready", "inv_ready", "attn_ready"))
        attnT_ready, achi_ready, aclo_ready = sem("attnT_ready"), sem("achi_ready"), sem("aclo_ready")
        y_ready, yhi_ready, ylo_ready, out_ready = (sem(n) for n in (
            "y_ready", "yhi_ready", "ylo_ready", "out_ready"))

        def is_pair(p):
            return not isinstance(p, int) or 0 <= p < PAIRS

        def is_period(t, number):
            return isinstance(t, int) and t == number

        def wait_pairs(eng, semaphore, count):
            if not isinstance(count, int) or count > 0:
                eng.wait_ge(semaphore, count)

        def run_periods(eng, period, behind, ahead, skip=0, before={}):
            first = behind + skip
            rounds = (PAIRS - ahead - first) // RING
            after = first + rounds * RING
            for t in range(-ahead, first):
                before.get(t, lambda: None)()
                period(t, t)
            with eng.Fori(first, after - RING + 1, RING) as base:
                for j in range(RING):
                    period(base + j, first + j)
            for t in range(after, PAIRS + behind):
                period(t, t)

        q_banks, bank_k, bank_v = ((bank_xT, bank_pT), (bank_ac, bank_y)), bank_cT, bank_f
        bank_m, bank_o, bank_fm = bank_u, bank_y, bank_f
        q_parts = [[q_banks[a][e][:, 0:KT * (P + 1)].rearrange("p (k n) -> p k n", k=KT) for e in range(KE)]
                   for a in range(2)]

        def bias_at(i, a, e):
            return (2 * i + a) * KE + e

        def yT_bank(p):
            if isinstance(p, int) and p >= PAIRS - 3:
                return (bank_xT, bank_cT, bank_xT)[p - (PAIRS - 3)]
            return bank_ac

        def is_last(p):
            return isinstance(p, int) and p == PAIRS - 1

        def y_bank(p, b):
            return (bank_y, bank_s)[b] if is_last(p) else bank_y

        def f_bank(p, b):
            return (bank_f, bank_pT)[b] if is_last(p) else bank_f

        block = es.enter_context(nc.Block())

        @block.sync
        def _(sp):
            sp.dma_start(cols[:, :], vector_cols).then_inc(cols_in, 16)
            for a in range(2):
                sp.dma_start(wq[:, a, :, :], w_q[a].rearrange("(k p) e -> p k e", p=P)).then_inc(wq_in[a], 16)

            def load(p, s):
                wait_pairs(sp, cn_ready, p - RING + 1)
                arrived = loaded[s % RING]
                sp.dma_start(x_all[:, bass.ds(p, 1), :, :], x_pairs[bass.ds(p, 1)].rearrange("p s b d -> s p b d")).then_inc(arrived, 16)
                sp.dma_start(raw[:, s % RING, 0, :, :], c_pairs[bass.ds(p, 1)].rearrange("p s b d -> s (p b) d")).then_inc(arrived, 16)
                sp.dma_start(raw[:, s % RING, 1, :, :], f_pairs[bass.ds(p, 1)].rearrange("p s b d -> s (p b) d")).then_inc(arrived, 16)

            def period(t, s):
                if is_last(t - 4):
                    for b, ready in enumerate((out_first_ready, out_ready)):
                        sp.wait_ge(ready, 1 if b == 0 else PAIRS)
                        sp.dma_start(out[2 * PAIRS - 2 + b], result[:, s % 2, b, :]).then_inc(stored[s % 2], 16)
                elif is_pair(t - 4):
                    sp.wait_ge(out_ready, t - 4 + 1)
                    sp.dma_start(out_pairs[bass.ds(t - 4, 1)].rearrange("p s b d -> s (p b) d"),
                                 result[:, s % 2, :, :]).then_inc(stored[s % 2], 16)
                if is_pair(t + 5):
                    load(t + 5, s + 5)

            def load_wkv():
                for i in range(2):
                    sp.dma_start(wkv[:, :, i, :], w_kv[:, i].rearrange("a p e -> p a e")).then_inc(wkv_in[i], 16)

            def load_wo():
                sp.dma_start(rows[:, :, :], bias_rows).then_inc(rows_in, 16)
                sp.dma_start(wo[:, :, :, :], w_o.rearrange("a (k p) d -> p a k d", p=P)).then_inc(wo_in, 16)

            def load_wf():
                sp.dma_start(wf[:, :, :], fc_w.rearrange("(k p) d -> p k d", p=P)).then_inc(wf_in, 16)

            run_periods(sp, period, 4, 5, before={-4: load_wkv, -3: load_wo, -2: load_wf})
            for s in range(2):
                sp.wait_ge(stored[s], 16 * (PAIRS // 2 + s))

        @block.gpsimd
        def _(pool):
            pool.memset(ident[:, :], 0.0).then_inc(ident_made, 1)
            pool.memset(eps[:, :], EPS)
            pool.memset(one[:, :], 1.0)
            pool.memset(minus_half[:, :], -0.5).then_inc(half_made, 1)
            pool.wait_ge(ident_made, 1)
            pool.affine_select(out=ident[:, :], in_=ident[:, :], compare_op=ALU.not_equal, fill=1.0,
                               base=0, pattern=[[-1, P]], channel_multiplier=1).then_inc(ident_made, 1)

            def norm_scalars(p, mv, mv_done, var_eps, var_done, rstd, rstd_done, prod, prod_done, offset, ready):
                pool.wait_ge(mv_done, p + 1)
                rows = var_eps.shape[1]
                pool.tensor_tensor(var_eps, mv[:, :, 1], eps[:, 0:rows], ALU.add).then_inc(var_done, 1)
                pool.wait_ge(var_done, p + 1)
                pool.tensor_tensor(rstd, var_eps, minus_half[:, 0:rows], ALU.pow).then_inc(rstd_done, 1)
                pool.wait_ge(rstd_done, p + 1)
                pool.tensor_tensor(prod, mv[:, :, 0], rstd, ALU.mult).then_inc(prod_done, 1)
                pool.wait_ge(prod_done, p + 1)
                pool.tensor_tensor(offset, one[:, 0:rows], prod, ALU.subtract).then_inc(ready, 1)

            def in_norm_scalars(p, w):
                norm_scalars(p, in_mv[:, w], in_mv_done, in_var_eps[:, w], in_var_done, in_rstd[:, w],
                             in_rstd_done, in_mean_rstd[:, w], in_prod_done, in_offset[:, w], in_norm_ready)

            def y_norm_scalars(p, w):
                norm_scalars(p, y_mv[:, w], y_mv_done, y_var_eps[:, w], y_var_done, y_rstd[:, w],
                             y_rstd_done, y_mean_rstd[:, w], y_prod_done, y_offset[:, w], y_norm_ready)

            pool.wait_ge(half_made, 1)

            def period(t, s):
                if is_pair(t + 2):
                    p, w = t + 2, s % 2
                    wait_pairs(pool, xn_ready, p - 1)
                    in_norm_scalars(p, w)
                    pool.wait_ge(in_norm_ready, p + 1)
                    wait_pairs(pool, ac_done, p - 3)
                if is_pair(t - 2):
                    y_norm_scalars(t - 2, s % 2)
                if is_pair(t + 2):
                    w, r = s % 2, (s + 2) % RING
                    for a in range(2):
                        for b in range(2):
                            i = 2 + 2 * a + b
                            last = pool.tensor_scalar(cn[:, r, a, b, :], raw[:, r, a, b, :], in_rstd[:, w, i:i + 1],
                                                      in_offset[:, w, i:i + 1], ALU.mult, ALU.add)
                    last.then_inc(cn_ready, 1)
                if is_pair(t) and not is_last(t):
                    w = s % 2
                    pool.wait_ge(inv_ready, t + 1)
                    wait_pairs(pool, pT_done, t - 1)
                    pool.tensor_tensor(attn[:, w], exps[:, w], inv_sum[:, w].unsqueeze(2).to_broadcast([P, 4, P]),
                                       ALU.mult).then_inc(attn_ready, 1)

            run_periods(pool, period, 2, 2)

        @block.scalar
        def _(act):
            def make_q2T():
                act.wait_ge(share_made, 2)
                for a in range(2):
                    act.wait_ge(q_turned, a + 1)
                    for e in range(KE):
                        act.activation(half_q[:, a, e:e + 1], q_parts[a][e][:, 0, P:P + 1], ACT.Identity,
                                       bias=bias_share[:, bias_at(0, a, e):bias_at(0, a, e) + 1]).then_inc(half_q_made, 1)
                    act.wait_ge(half_q_made, KE * (a + 1))
                    for e in range(KE):
                        act.activation(added_q[:, a, e:e + 1], q_parts[a][e][:, 1, P:P + 1], ACT.Identity,
                                       bias=half_q[:, a, e:e + 1]).then_inc(added_q_made, 1)
                    act.wait_ge(added_q_made, KE * (a + 1))
                    for e in range(KE):
                        act.activation(q2T[:, a, e, :].rearrange("p (k n) -> p k n", k=KT), q_parts[a][e][:, :, 0:P],
                                       ACT.Identity, bias=added_q[:, a, e:e + 1]).then_inc(q2T_made, 1)

            def make_m_hi():
                act.wait_ge(m_made, 1)
                act.activation(flat(m_hi), bank_m[:, :], ACT.Copy, scale=SCALE).then_inc(hi_made, 1)

            def make_v2T():
                act.wait_ge(v_turned, 1)
                for a in range(2):
                    for e in range(KE):
                        at = (a * KE + e) * P
                        act.activation(v2T[:, a, e, :], bank_v[:, at:at + P], ACT.Identity,
                                       bias=bias_share[:, bias_at(2, a, e):bias_at(2, a, e) + 1]).then_inc(v2T_made, 1)

            def make_o_hi():
                act.wait_ge(o_made, 2)
                act.activation(flat(o_hi), bank_o[:, :], ACT.Copy).then_inc(hi_made, 1)

            def make_f_hi():
                act.wait_ge(f_folded, 1)
                act.activation(flat(f_hi), flat(f2), ACT.Copy).then_inc(hi_made, 1)

            act.wait_ge(consts_made, 1)
            act.activation(first_exp[:, :], mean_dt[:, 0:1], ACT.Exp)

            def yn_high(t, v):
                act.wait_ge(yT_done, t - 3 + 1)
                act.activation(flat(yT_hi[v]), yT_bank(t - 3)[:, :], ACT.Copy).then_inc(yhi_ready, 1)

            def xn_high(t, v):
                act.wait_ge(xT_done, t + 1 + 1)
                wait_pairs(act, u_done, t + 1 - 1)
                act.activation(flat(xT_hi[v]), bank_xT[:, :], ACT.Copy).then_inc(xhi_ready, 1)

            def take_attnT(t, v):
                act.wait_ge(pT_done, t - 1 + 1)
                wait_pairs(act, ac_done, t - 1 - 1)
                act.activation(flat(attnT[:, v]), bank_pT[:, :], ACT.Copy).then_inc(attnT_ready, 1)

            def take_cT(t, v):
                act.wait_ge(cT_done, t + 1 + 1)
                wait_pairs(act, s_done, t + 1 - 1)
                act.activation(flat(cT[:, v]), bank_cT[:, :], ACT.Copy).then_inc(cT_ready, 1)

            def normalise_x(t, w):
                act.wait_ge(in_norm_ready, t + 2 + 1)
                wait_pairs(act, xT_done, t + 2 - 1)
                for b in range(2):
                    last = act.activation(xn[:, w, b, :], x_all[:, bass.ds(t + 2, 1), b, :], ACT.Identity,
                                          bias=in_offset[:, w, b:b + 1], scale=in_rstd[:, w, b:b + 1])
                last.then_inc(xn_ready, 1)

            def ac_high(t, v):
                act.wait_ge(ac_done, t - 1 + 1)
                wait_pairs(act, y_done, t - 1 - 1)
                act.activation(flat(acT_hi[v]), bank_ac[:, :], ACT.Copy).then_inc(achi_ready, 1)

            def exponentials(t, w):
                act.wait_ge(max_ready, t + 1)
                wait_pairs(act, attn_ready, t - 1)
                for i in range(4):
                    last = act.activation(exps[:, w, i, :], bank_s[:, i * P:(i + 1) * P], ACT.Exp,
                                          bias=neg_max[:, w, i:i + 1], accum_out=exp_sum[:, w, i:i + 1])
                last.then_inc(exp_ready, 1)

            def take_uT(t, v):
                act.wait_ge(u_done, t + 1 + 1)
                wait_pairs(act, s_done, t + 1 - 1)
                act.activation(flat(uT[:, v]), bank_u[:, :], ACT.Copy).then_inc(uT_ready, 1)

            def normalise_y(t, s):
                w = s % 2
                act.wait_ge(y_norm_ready, t - 2 + 1)
                for b in range(1 if is_last(t - 2) else 2):
                    last = act.activation(yn[:, w, b, :], y[:, (s - 2) % RING, b, :], ACT.Identity,
                                          bias=y_offset[:, w, b:b + 1], scale=y_rstd[:, w, b:b + 1])
                last.then_inc(yn_ready, 1)

            def period(t, s):
                w, v = s % 2, (s + 1) % 2
                early = is_period(t, 0) or is_period(t, 1)
                last, after_last = is_last(t), is_period(t, PAIRS)
                if is_pair(t - 3) and not after_last:
                    yn_high(t, v)
                if is_pair(t + 1):
                    xn_high(t, v)
                if is_period(t, -1):
                    make_m_hi()
                if is_period(t, 1):
                    make_f_hi()
                if is_pair(t - 1):
                    take_attnT(t, v)
                if is_period(t, 1):
                    make_o_hi()
                if is_pair(t + 1):
                    take_cT(t, v)
                if last:
                    exponentials(t, w)
                if is_pair(t + 2) and not early:
                    normalise_x(t, w)
                if is_pair(t - 1):
                    ac_high(t, v)
                if is_pair(t - 3) and after_last:
                    yn_high(t, v)
                if is_pair(t) and not last:
                    exponentials(t, w)
                if is_pair(t + 2) and early:
                    normalise_x(t, w)
                if is_period(t, 2):
                    normalise_y(t, s)
                if is_pair(t + 1):
                    take_uT(t, v)
                if is_pair(t - 2) and not is_period(t, 2):
                    normalise_y(t, s)

            run_periods(act, period, 3, 2, before={-2: make_q2T, -1: make_v2T})

        @block.vector
        def _(dve):
            dve.memset(mean_dt[:, :], 1.0 / DT)
            dve.memset(mean_dc[:, :], 1.0 / P).then_inc(consts_made, 1)
            dve.wait_ge(cols_in, 16)
            dve.tensor_tensor(shift_less_gain[:, :], cols[:, NORMS:2 * NORMS], cols[:, 0:NORMS],
                              ALU.subtract).then_inc(diff_made, 1)

            dve.wait_ge(ident_made, 2)
            dve.wait_ge(diff_made, 1)
            for a in range(2):
                for k in range(KT):
                    dve.tensor_scalar(turn_q[:, a, k, 0:P], ident[:, :], cols[:, LN1[a] + k:LN1[a] + k + 1], None, ALU.mult)
                last = dve.tensor_scalar(turn_q[:, a, :, P], shift_less_gain[:, LN1[a]:LN1[a] + KT], 1.0 / DT, None, ALU.mult)
            last.then_inc(turn_q_made, 1)
            for a in range(2):
                last = dve.tensor_scalar(share_kv[:, a:a + 1], shift_less_gain[:, LN2[a]:LN2[a] + 1], 1.0 / P, None, ALU.mult)
            last.then_inc(share_made, 1)
            dve.tensor_scalar(bias_share[:, 0:2 * KE], bias_cols[:, 0:2 * KE], 1.0 / DT, None, ALU.mult)
            dve.tensor_scalar(bias_share[:, 2 * KE:], bias_cols[:, 2 * KE:], 1.0 / P, None, ALU.mult).then_inc(share_made, 1)
            dve.wait_ge(share_made, 1)
            for a in range(2):
                last = dve.tensor_scalar(turn_kv[:, a, :], ident[:, :], cols[:, LN2[a]:LN2[a] + 1],
                                         share_kv[:, a:a + 1], ALU.mult, ALU.add)
            last.then_inc(turn_kv_made, 1)

            def make_k2T():
                dve.wait_ge(share_made, 2)
                dve.wait_ge(k_turned, 1)
                for a in range(2):
                    for e in range(KE):
                        at = (a * KE + e) * P
                        last = dve.tensor_scalar(k2T[:, a, e, :], bank_k[:, at:at + P],
                                                 bias_share[:, bias_at(1, a, e):bias_at(1, a, e) + 1], None, ALU.add)
                    last.then_inc(k2T_made, 1)

            def make_m_lo():
                dve.wait_ge(hi_made, 1)
                dve.scalar_tensor_tensor(flat(m_lo), bank_m[:, :], SCALE, flat(m_hi).bitcast(FP32),
                                         ALU.mult, ALU.subtract).then_inc(lo_made, 1)

            def scale_f():
                dve.wait_ge(wf_in, 16)
                for k in range(KT):
                    last = dve.tensor_scalar(scaled_f[:, k, :], wf[:, k, :],
                                             shift_less_gain[:, LNF + k:LNF + k + 1], None, ALU.mult)
                last.then_inc(f_scaled, 1)

            def fold_f():
                dve.wait_ge(f_means_made, 1)
                for k in range(KT):
                    last = dve.scalar_tensor_tensor(f2[:, k, :], wf[:, k, :], cols[:, LNF + k:LNF + k + 1],
                                                    bank_fm[:, 0:DT], ALU.mult, ALU.add)
                last.then_inc(f_folded, 1)

            def make_o_lo():
                dve.wait_ge(hi_made, 3)
                dve.tensor_tensor(flat(o_lo), bank_o[:, :], flat(o_hi).bitcast(FP32), ALU.subtract).then_inc(lo_made, 1)

            def make_f_lo():
                dve.wait_ge(hi_made, 2)
                dve.tensor_tensor(flat(f_lo), flat(f2), flat(f_hi).bitcast(FP32), ALU.subtract).then_inc(lo_made, 1)

            def find_maxima(t, w):
                dve.wait_ge(s_done, t + 1)
                wait_pairs(dve, exp_ready, t - 1)
                dve.tensor_reduce(neg_max[:, w], bank_s[:, :].rearrange("p (i k) -> p i k", i=4), AX.X, ALU.max,
                                  negate=True).then_inc(max_ready, 1)

            def yn_low(t, v):
                dve.wait_ge(yhi_ready, t - 3 + 1)
                dve.tensor_tensor(flat(yT_lo[v]), yT_bank(t - 3)[:, :], flat(yT_hi[v]).bitcast(FP32),
                                  ALU.subtract).then_inc(ylo_ready, 1)

            def ac_low(t, v):
                dve.wait_ge(achi_ready, t - 1 + 1)
                dve.tensor_tensor(flat(acT_lo[v]), bank_ac[:, :], flat(acT_hi[v]).bitcast(FP32),
                                  ALU.subtract).then_inc(aclo_ready, 1)

            def invert_sums(t, w):
                dve.wait_ge(exp_ready, t + 1)
                wait_pairs(dve, attn_ready, t - 1)
                dve.reciprocal(inv_sum[:, w], exp_sum[:, w]).then_inc(inv_ready, 1)

            def aggregate_y(w):
                for b in range(2):
                    last = dve.bn_aggr(y_mv[:, w, b, :], y_bn[:, w, b, :])
                last.then_inc(y_mv_done, 1)

            def period(t, s):
                w, v, r = s % 2, (s + 1) % 2, s % RING
                after_last = is_period(t, PAIRS)
                last_max = is_last(t)
                last_y = is_last(t - 2)
                if after_last:
                    ac_low(t, v)
                if is_pair(t - 2):
                    dve.wait_ge(y_bn_done, t - 2 + 1)
                    wait_pairs(dve, y_norm_ready, t - 2 - 1)
                if is_pair(t - 2) and (after_last or last_y):
                    aggregate_y(w)
                if is_pair(t - 4):
                    p = t - 4
                    if is_last(p):
                        dve.wait_ge(f_first_done, 1)
                    else:
                        dve.wait_ge(f_done, p + 1)
                    wait_pairs(dve, stored[w], 8 * (p - w))
                    if is_last(p):
                        for b, ready in enumerate((out_first_ready, out_ready)):
                            if b == 1:
                                dve.wait_ge(f_done, PAIRS)
                            dve.tensor_tensor(result[:, w, b, :], f_bank(p, b)[:, b * DT:(b + 1) * DT], y[:, r, b, :],
                                              ALU.add).then_inc(ready, 1)
                    else:
                        dve.tensor_tensor(flat(result[:, w]), bank_f[:, :], flat(y[:, r]), ALU.add).then_inc(out_ready, 1)
                if is_pair(t - 2) and not (after_last or last_y):
                    aggregate_y(w)
                if is_pair(t - 3) and not after_last:
                    yn_low(t, v)
                if last_y:
                    dve.wait_ge(y_norm_ready, PAIRS)
                    dve.tensor_scalar(yn[:, w, 1, :], y[:, (s - 2) % RING, 1, :], y_rstd[:, w, 1:2], y_offset[:, w, 1:2],
                                      ALU.mult, ALU.add).then_inc(yn_second_ready, 1)
                if is_pair(t + 1):
                    dve.wait_ge(xhi_ready, t + 1 + 1)
                    dve.tensor_tensor(flat(xT_lo[v]), bank_xT[:, :], flat(xT_hi[v]).bitcast(FP32),
                                      ALU.subtract).then_inc(xlo_ready, 1)
                if is_period(t, -1):
                    make_m_lo()
                if is_period(t, 1):
                    make_f_lo()
                if is_pair(t):
                    find_maxima(t, w)
                if is_period(t, 1):
                    make_o_lo()
                if is_pair(t + 3):
                    dve.wait_ge(loaded[(s + 3) % RING], 12 * (t + 3 - (s + 3) % RING) + 48)
                    for b in range(2):
                        dve.bn_stats(in_bn[:, v, b, :], x_all[:, bass.ds(t + 3, 1), b, :])
                if last_max:
                    invert_sums(t, w)
                    dve.wait_ge(inv_ready, PAIRS)
                    dve.wait_ge(pT_done, t - 1)
                    dve.tensor_tensor(attn[:, w], exps[:, w], inv_sum[:, w].unsqueeze(2).to_broadcast([P, 4, P]),
                                      ALU.mult).then_inc(attn_ready, 1)
                if is_pair(t - 1) and not after_last:
                    ac_low(t, v)
                if after_last:
                    yn_low(t, v)
                if is_pair(t + 3):
                    for i in range(4):
                        last = dve.bn_stats(in_bn[:, v, 2 + i, :], raw[:, (s + 3) % RING, i // 2, i % 2, :])
                    last.then_inc(in_bn_done, 1)
                    wait_pairs(dve, in_norm_ready, t + 3 - 1)
                    dve.wait_ge(in_bn_done, t + 3 + 1)
                if is_pair(t) and not last_max:
                    invert_sums(t, w)
                if is_pair(t + 3):
                    for i in range(6):
                        last = dve.bn_aggr(in_mv[:, v, i, :], in_bn[:, v, i, :])
                    last.then_inc(in_mv_done, 1)
                if is_pair(t - 1):
                    p = t - 1
                    if is_last(p):
                        for b, done in enumerate((y_first_done, y_done)):
                            dve.wait_ge(done, 1 if b == 0 else PAIRS)
                            dve.tensor_tensor(y[:, p % RING, b, :], y_bank(p, b)[:, b * DT:(b + 1) * DT], x_all[:, p, b, :],
                                              ALU.add).then_inc(y_ready, 1)
                            dve.wait_ge(y_ready, p + 1 + b)
                            last = dve.bn_stats(y_bn[:, v, b, :], y[:, p % RING, b, :])
                    else:
                        dve.wait_ge(y_done, p + 1)
                        dve.tensor_tensor(y[:, (s - 1) % RING], bank_y[:, :].rearrange("p (b d) -> p b d", b=2),
                                          x_all[:, bass.ds(p, 1), :, :].rearrange("p o b d -> p (o b) d"),
                                          ALU.add).then_inc(y_ready, 1)
                        dve.wait_ge(y_ready, p + 1)
                        for b in range(2):
                            last = dve.bn_stats(y_bn[:, v, b, :], y[:, (s - 1) % RING, b, :])
                    last.then_inc(y_bn_done, 1)

            run_periods(dve, period, 4, 3, skip=2, before={-2: make_k2T, 0: scale_f, 1: fold_f})

        @block.tensor
        def _(pe):
            pe.wait_ge(ident_made, 2)
            for _ in range(WARM_UP):
                pe.transpose(bank_f[:, 0:P], ident[:, :], ident[:, :])
            pe.wait_ge(turn_q_made, 1)
            for a in range(2):
                pe.wait_ge(wq_in[a], 16)
                for e in range(KE):
                    for k in range(KT):
                        last = pe.matmul(q_parts[a][e][:, k, :], wq[:, a, k, e * P:(e + 1) * P], turn_q[:, a, k, :],
                                         start=True, stop=True)
                last.then_inc(q_turned, 1)

            def turn(i, bank, done):
                pe.wait_ge(wkv_in[i], 16)
                for a in range(2):
                    for e in range(KE):
                        at = (a * KE + e) * P
                        last = pe.matmul(bank[:, at:at + P], wkv[:, a, i, e * P:(e + 1) * P], turn_kv[:, a, :],
                                         start=True, stop=True)
                last.then_inc(done, 1)

            pe.wait_ge(turn_kv_made, 1)
            turn(0, bank_k, k_turned)
            turn(1, bank_v, v_turned)
            for a in range(2):
                pe.wait_ge(k2T_made, a + 1)
                pe.wait_ge(q2T_made, KE * (a + 1))
                for k in range(KT):
                    at = (a * KT + k) * P
                    for e in range(KE):
                        last = pe.matmul(bank_m[:, at:at + P], q2T[:, a, e, k * P:(k + 1) * P], k2T[:, a, e, :],
                                         start=(e == 0), stop=(e == KE - 1))
            last.then_inc(m_made, 1)

            def make_f_means():
                pe.wait_ge(consts_made, 1)
                pe.wait_ge(rows_in, 16)
                pe.wait_ge(f_scaled, 1)
                for k in range(KT):
                    pe.matmul(bank_fm[:, 0:DT], mean_dt[:, :], scaled_f[:, k, :], start=(k == 0), stop=False)
                pe.matmul(bank_fm[:, 0:DT], mean_dt[0:1, :], rows[0:1, BFC, :], start=False,
                          stop=True).then_inc(f_means_made, 1)

            def make_o(a):
                pe.wait_ge(rows_in, 16)
                pe.wait_ge(wo_in, 16)
                pe.wait_ge(v2T_made, KE * (a + 1))
                o = bank_o[:, a * DT:(a + 1) * DT]
                for e in range(KE):
                    pe.matmul(o, v2T[:, a, e, :], wo[:, a, e, :], start=(e == 0), stop=False)
                pe.matmul(o, mean_dc[0:1, :], rows[0:1, BO[a], :], start=False, stop=True).then_inc(o_made, 1)

            def make_f_means_o():
                make_f_means()
                make_o(1)

            def turn_attn(p, slot):
                pe.wait_ge(attn_ready, p + 1)
                wait_pairs(pe, attnT_ready, p)
                for i in range(4):
                    last = pe.transpose(bank_pT[:, i * P:(i + 1) * P], attn[:, slot, i, :], ident[:, :])
                last.then_inc(pT_done, 1)

            def dense(p, slot):
                pe.wait_ge(yhi_ready, p + 1)
                wait_pairs(pe, out_ready, p)

                def high(b):
                    for k in range(KT):
                        o = f_bank(p, b)[:, b * DT:(b + 1) * DT]
                        pe.matmul(o, yT_hi[slot][:, k, b, :], f_hi[:, k, :], start=(k == 0), stop=False)
                        pe.matmul(o, yT_hi[slot][:, k, b, :], f_lo[:, k, :], start=False, stop=False)

                high(0)
                if is_last(p):
                    high(1)
                pe.wait_ge(ylo_ready, p + 1)
                for b in range(2):
                    if b == 1 and not is_last(p):
                        high(1)
                    for k in range(KT):
                        last = pe.matmul(f_bank(p, b)[:, b * DT:(b + 1) * DT], yT_lo[slot][:, k, b, :], f_hi[:, k, :],
                                         start=False, stop=(k == KT - 1))
                    if b == 0 and is_last(p):
                        last.then_inc(f_first_done, 1)
                last.then_inc(f_done, 1)

            def turn_yn(p, slot):
                pe.wait_ge(yn_ready, p + 1)
                if is_last(p):
                    pe.wait_ge(yn_second_ready, 1)
                if yT_bank(p) is bank_ac:
                    wait_pairs(pe, aclo_ready, p + 2)
                elif p == PAIRS - 3:
                    pe.wait_ge(xlo_ready, PAIRS)
                elif p == PAIRS - 2:
                    pe.wait_ge(cT_ready, PAIRS)
                else:
                    pe.wait_ge(ylo_ready, PAIRS - 2)
                for k in range(KT):
                    for b in range(2):
                        at = (2 * k + b) * P
                        last = pe.transpose(yT_bank(p)[:, at:at + P], yn[:, slot, b, k * P:(k + 1) * P], ident[:, :])
                last.then_inc(yT_done, 1)

            def period(t, s):
                w, v = s % 2, (s + 1) % 2
                if is_pair(t + 1):
                    p = t + 1
                    pe.wait_ge(xn_ready, p + 1)
                    wait_pairs(pe, xlo_ready, p)
                    for k in range(KT):
                        for b in range(2):
                            at = (2 * k + b) * P
                            last = pe.transpose(bank_xT[:, at:at + P], xn[:, v, b, k * P:(k + 1) * P], ident[:, :])
                    last.then_inc(xT_done, 1)
                if is_pair(t - 1) and not is_last(t - 1):
                    turn_attn(t - 1, v)
                if is_pair(t + 1):
                    p, r = t + 1, (s + 1) % RING
                    pe.wait_ge(cn_ready, p + 1)
                    wait_pairs(pe, cT_ready, p)
                    for a in range(2):
                        for b in range(2):
                            at = (2 * a + b) * P
                            last = pe.transpose(bank_cT[:, at:at + P], cn[:, r, a, b, :], ident[:, :])
                    last.then_inc(cT_done, 1)
                if is_period(t, -1):
                    make_o(0)
                if is_pair(t):
                    pe.wait_ge(cT_ready, t + 1)
                    pe.wait_ge(uT_ready, t + 1)
                    wait_pairs(pe, exp_ready, t)
                    for a in range(2):
                        for b in range(2):
                            at = (2 * a + b) * P
                            last = pe.matmul(bank_s[:, at:at + P], uT[:, w, a, b, :], cT[:, w, a, b, :],
                                             start=True, stop=True)
                    last.then_inc(s_done, 1)
                if is_pair(t - 1):
                    pe.wait_ge(attnT_ready, t - 1 + 1)
                    if is_period(t, PAIRS):
                        pe.wait_ge(aclo_ready, t - 1)
                    else:
                        wait_pairs(pe, ylo_ready, t - 2)
                    for i in range(4):
                        last = pe.matmul(bank_ac[:, i * P:(i + 1) * P], cn[:, (s - 1) % RING, i // 2, i % 2, :],
                                         attnT[:, v, i, :], start=True, stop=True)
                    last.then_inc(ac_done, 1)
                if is_last(t):
                    dense(t - 3, v)
                    turn_attn(t, w)
                if is_period(t, PAIRS):
                    turn_yn(t - 3, v)
                if is_period(t, -1):
                    pe.wait_ge(lo_made, 1)
                if is_pair(t + 1):
                    pe.wait_ge(xhi_ready, t + 1 + 1)
                    wait_pairs(pe, uT_ready, t + 1)
                    for a in range(2):
                        u = bank_u[:, a * 2 * P:(a + 1) * 2 * P]
                        for k in range(KT):
                            pe.matmul(u, m_hi[:, a, k, :], xT_hi[v][:, k, :], start=(k == 0), stop=False)
                            pe.matmul(u, m_lo[:, a, k, :], xT_hi[v][:, k, :], start=False, stop=False)
                        if a == 0:
                            pe.wait_ge(xlo_ready, t + 1 + 1)
                        for k in range(KT):
                            last = pe.matmul(u, m_hi[:, a, k, :], xT_lo[v][:, k, :], start=False, stop=(k == KT - 1))
                    last.then_inc(u_done, 1)
                if is_period(t, 1):
                    pe.wait_ge(lo_made, 3)
                if is_pair(t - 1):
                    pe.wait_ge(achi_ready, t - 1 + 1)
                    wait_pairs(pe, y_ready, t - 1)
                    for b in range(2):
                        o = y_bank(t - 1, b)[:, b * DT:(b + 1) * DT]
                        for a in range(2):
                            pe.matmul(o, acT_hi[v][:, 2 * a + b, :], o_hi[:, a, :], start=(a == 0), stop=False)
                            pe.matmul(o, acT_hi[v][:, 2 * a + b, :], o_lo[:, a, :], start=False, stop=False)
                        if b == 0:
                            pe.wait_ge(aclo_ready, t - 1 + 1)
                        for a in range(2):
                            last = pe.matmul(o, acT_lo[v][:, 2 * a + b, :], o_hi[:, a, :], start=False, stop=(a == 1))
                        if b == 0 and is_period(t, PAIRS):
                            last.then_inc(y_first_done, 1)
                    last.then_inc(y_done, 1)
                if is_pair(t - 3) and not is_last(t):
                    dense(t - 3, v)
                if is_pair(t - 2) and not is_last(t):
                    turn_yn(t - 2, w)

            run_periods(pe, period, 3, 1, skip=1, before={1: make_f_means_o})


def flat(ap):
    ap = ap[:]
    names = " ".join("abcdef"[:len(ap.shape) - 1])
    return ap.rearrange(f"p {names} -> p ({names})") if len(ap.shape) > 2 else ap


def kernel(**inputs):
    import numpy as _np
    import concourse.bacc as _bacc
    from concourse import mybir as _mybir
    from concourse.bass_utils import run_bass_kernel_spmd as _run

    given = {n.removeprefix("L0_xattn_"): _np.asarray(a) for n, a in inputs.items()}
    norms = ("a_ln1", "a_ln2", "v_ln1", "v_ln2", "ln")
    vectors = [given[f"{n}_{k}"].reshape(-1, 128) for k in "gb" for n in norms]
    vectors += [given[f"{a}_{b}"].reshape(-1, 128) for b in ("bq", "bk", "bv") for a in "av"]
    laid = {
        "x": given["x"], "ctx": given["ctx_512"], "fside": given["fside_BxSxS_0"],
        "Wq": _np.stack([given[f"{a}_Wq"] for a in "av"]),
        "Wkv": _np.stack([_np.stack([given[f"{a}_Wk"], given[f"{a}_Wv"]]) for a in "av"]),
        "Wo": _np.stack([given[f"{a}_Wo"] for a in "av"]),
        "fc_W": given["fc_W"],
        "vector_cols": _np.concatenate(vectors, axis=0).T,
        "bias_rows": _np.stack([given["a_bo"], given["v_bo"], given["fc_b"]])[None],
    }

    nc = _bacc.Bacc("TRN2", target_bir_lowering=False, num_devices=1)
    arrays, args = {}, []
    for name, a in laid.items():
        a = _np.ascontiguousarray(a)
        arrays[f"in_{name}"] = a
        args.append(nc.dram_tensor(f"in_{name}", a.shape, _mybir.dt.from_np(a.dtype), kind="ExternalInput").ap())
    shape = laid["x"].shape
    args.append(nc.dram_tensor("out_0", shape, _mybir.dt.from_np(laid["x"].dtype), kind="ExternalOutput").ap())
    xattn_kernel(nc, *args)
    r = _run(nc, [arrays], core_ids=[0])
    return r.results[0]["out_0"]
```
